# Optimizing a Trainium2 kernel written in Bass

```python
import numpy as np
import jax
import jax.numpy as jnp

def _softmax(x, axis=-1):
    return jax.nn.softmax(x, axis=axis)

def _gelu(x):
    return jax.nn.gelu(x, approximate=True)

def _silu(x):
    return jax.nn.silu(x)

def _sigmoid(x):
    return jax.nn.sigmoid(x)

def _layernorm(x, axis=-1, eps=1e-05):
    m = jnp.mean(x, axis=axis, keepdims=True)
    v = jnp.var(x, axis=axis, keepdims=True)
    return (x - m) / jnp.sqrt(v + eps)

def _scatter_add(tgt, idx, src, axis=0):
    return tgt.at[idx].add(src)

def _segment_sum(src, seg, n):
    return jax.ops.segment_sum(src, seg, n)
kernel_name = 'mk_seq_preln_d1_jaxref_r4_71c0b6'

def setup_inputs(seed: int=0):
    np.random.seed(seed)
    _w = jnp.asarray

    def _L0_attn_setup():
        import jax, jax.numpy as jnp
        import numpy as np
        D_MODEL = 256
        N_HEADS = 16
        N_KV_HEADS = 4
        HEAD_DIM = 64
        S = 4
        W = 64
        B = 2
        T = 512

        def _sink_mask(seq_len, sink, window):
            t = jnp.arange(seq_len)
            i = t[:, None]
            j = t[None, :]
            sink_band = j < min(sink, seq_len)
            window_band = j >= jnp.maximum(i - window + 1, 0)
            causal = j <= i
            return causal & (sink_band | window_band)
        key = jax.random.key(seed)
        ks = jax.random.split(key, 5)
        scale = 0.02
        X = jax.random.normal(ks[0], (B, T, D_MODEL), dtype=jnp.float32)
        Wq = jax.random.normal(ks[1], (D_MODEL, N_HEADS * HEAD_DIM), dtype=jnp.float32) * scale
        Wk = jax.random.normal(ks[2], (D_MODEL, N_KV_HEADS * HEAD_DIM), dtype=jnp.float32) * scale
        Wv = jax.random.normal(ks[3], (D_MODEL, N_KV_HEADS * HEAD_DIM), dtype=jnp.float32) * scale
        Wo = jax.random.normal(ks[4], (N_HEADS * HEAD_DIM, D_MODEL), dtype=jnp.float32) * scale
        return {'X': X, 'Wq': Wq, 'Wk': Wk, 'Wv': Wv, 'Wo': Wo}
    _L0_attn_in = _L0_attn_setup()

    def _L0_ffn_setup():
        import jax, jax.numpy as jnp
        import numpy as np
        LN_EPS = 1e-05

        def layer_norm(x, g, b):
            mu = jnp.mean(x, axis=-1, keepdims=True)
            var = jnp.mean(jnp.square(x - mu), axis=-1, keepdims=True)
            return (x - mu) * jax.lax.rsqrt(var + LN_EPS) * g + b

        def ternary_quant(w):
            scale = 1.0 / jnp.clip(jnp.mean(jnp.abs(w)), 1e-05)
            wq = jnp.clip(jnp.round(w * scale), -1.0, 1.0) / scale
            return w + jax.lax.stop_gradient(wq - w)
        key = jax.random.key(seed)
        ks = jax.random.split(key, 3)
        dim, hidden = (256, 1024)
        B, S = (8, 256)
        x = jax.random.normal(ks[0], (B, S, dim), dtype=jnp.float32)
        w1 = jax.random.normal(ks[1], (hidden, dim), dtype=jnp.float32) * 0.02
        w2 = jax.random.normal(ks[2], (dim, hidden), dtype=jnp.float32) * 0.02
        return {'x': x, 'ln1_g': jnp.ones((dim,), jnp.float32), 'ln1_b': jnp.zeros((dim,), jnp.float32), 'w1': w1, 'b1': jnp.zeros((hidden,), jnp.float32), 'ln2_g': jnp.ones((hidden,), jnp.float32), 'ln2_b': jnp.zeros((hidden,), jnp.float32), 'w2': w2, 'b2': jnp.zeros((dim,), jnp.float32)}
    _L0_ffn_in = _L0_ffn_setup()
    _d = {'L0_attn_X': _L0_attn_in['X'], 'L0_attn_Wq': _L0_attn_in['Wq'], 'L0_attn_Wk': _L0_attn_in['Wk'], 'L0_attn_Wv': _L0_attn_in['Wv'], 'L0_attn_Wo': _L0_attn_in['Wo'], 'L0_ffn_ln1_g': _L0_ffn_in['ln1_g'], 'L0_ffn_ln1_b': _L0_ffn_in['ln1_b'], 'L0_ffn_w1': _L0_ffn_in['w1'], 'L0_ffn_b1': _L0_ffn_in['b1'], 'L0_ffn_ln2_g': _L0_ffn_in['ln2_g'], 'L0_ffn_ln2_b': _L0_ffn_in['ln2_b'], 'L0_ffn_w2': _L0_ffn_in['w2'], 'L0_ffn_b2': _L0_ffn_in['b2']}
    _x0 = _d['L0_attn_X']
    _d['L0_attn_X'] = jax.random.normal(jax.random.fold_in(jax.random.key(seed), 1), (8, 512, 256), dtype=_x0.dtype)
    del _x0
    return _d

def reference(L0_attn_X, L0_attn_Wq, L0_attn_Wk, L0_attn_Wv, L0_attn_Wo, L0_ffn_ln1_g, L0_ffn_ln1_b, L0_ffn_w1, L0_ffn_b1, L0_ffn_ln2_g, L0_ffn_ln2_b, L0_ffn_w2, L0_ffn_b2):

    def _L0_attn_ref(X, Wq, Wk, Wv, Wo):
        import jax, jax.numpy as jnp
        import numpy as np
        D_MODEL = 256
        N_HEADS = 16
        N_KV_HEADS = 4
        HEAD_DIM = 64
        S = 4
        W = 64
        B = 2
        T = 512

        def _sink_mask(seq_len, sink, window):
            t = jnp.arange(seq_len)
            i = t[:, None]
            j = t[None, :]
            sink_band = j < min(sink, seq_len)
            window_band = j >= jnp.maximum(i - window + 1, 0)
            causal = j <= i
            return causal & (sink_band | window_band)
        b, t, _ = X.shape
        d = HEAD_DIM
        Q = (X @ Wq).reshape(b, t, N_HEADS, d)
        K = (X @ Wk).reshape(b, t, N_KV_HEADS, d)
        V = (X @ Wv).reshape(b, t, N_KV_HEADS, d)
        rep = N_HEADS // N_KV_HEADS
        K = jnp.repeat(K, rep, axis=2)
        V = jnp.repeat(V, rep, axis=2)
        scale = 1.0 / np.sqrt(d)
        logits = jnp.einsum('bthd,bshd->bhts', Q * scale, K)
        M = _sink_mask(t, S, W)[None, None]
        neg = jnp.finfo(logits.dtype).min
        masked = jnp.where(M, logits, neg)
        mx = jnp.max(masked, axis=-1, keepdims=True)
        exp = jnp.exp(masked - mx) * M.astype(logits.dtype)
        denom = jnp.maximum(jnp.sum(exp, axis=-1, keepdims=True), jnp.finfo(logits.dtype).tiny)
        P = exp / denom
        Y = jnp.einsum('bhts,bshd->bthd', P, V)
        return Y.reshape(b, t, N_HEADS * d) @ Wo

    def _L0_ffn_ref(x, ln1_g, ln1_b, w1, b1, ln2_g, ln2_b, w2, b2):
        import jax, jax.numpy as jnp
        import numpy as np
        LN_EPS = 1e-05

        def layer_norm(x, g, b):
            mu = jnp.mean(x, axis=-1, keepdims=True)
            var = jnp.mean(jnp.square(x - mu), axis=-1, keepdims=True)
            return (x - mu) * jax.lax.rsqrt(var + LN_EPS) * g + b

        def ternary_quant(w):
            scale = 1.0 / jnp.clip(jnp.mean(jnp.abs(w)), 1e-05)
            wq = jnp.clip(jnp.round(w * scale), -1.0, 1.0) / scale
            return w + jax.lax.stop_gradient(wq - w)
        h = layer_norm(x, ln1_g, ln1_b)
        h = jnp.einsum('bsd,hd->bsh', h, ternary_quant(w1)) + b1
        h = jax.nn.gelu(h, approximate=False)
        h = layer_norm(h, ln2_g, ln2_b)
        out = jnp.einsum('bsh,dh->bsd', h, ternary_quant(w2)) + b2
        return out
    x = L0_attn_X
    x = x + _L0_attn_ref(_layernorm(x, axis=-1), L0_attn_Wq, L0_attn_Wk, L0_attn_Wv, L0_attn_Wo)
    x = x + _L0_ffn_ref(_layernorm(x, axis=-1), L0_ffn_ln1_g, L0_ffn_ln1_b, L0_ffn_w1, L0_ffn_b1, L0_ffn_ln2_g, L0_ffn_ln2_b, L0_ffn_w2, L0_ffn_b2)
    return x

_drawn_inputs = setup_inputs


def setup_inputs(seed=0):
    import zlib

    import numpy as np

    out = dict(_drawn_inputs(seed))
    spreads = {'L0_ffn_ln1_g': (1.0, 0.2),
     'L0_ffn_ln1_b': (0.0, 0.1),
     'L0_ffn_b1': (0.0, 0.1),
     'L0_ffn_ln2_g': (1.0, 0.2),
     'L0_ffn_ln2_b': (0.0, 0.1),
     'L0_ffn_b2': (0.0, 0.1)}
    factors = {'L0_attn_Wq': 8.0, 'L0_attn_Wk': 8.0}
    for name, (base, spread) in spreads.items():
        noise = np.random.default_rng([zlib.crc32(name.encode()), seed]).standard_normal(out[name].shape)
        drawn = base * np.exp(spread * noise) if base else spread * noise
        out[name] = jnp.asarray(drawn.astype(out[name].dtype))
    for name, factor in factors.items():
        out[name] = (out[name] * factor).astype(out[name].dtype)
    return out
```

```python
from contextlib import ExitStack

import concourse.bass as bass
from concourse import mybir

P = 128
F32 = mybir.dt.float32
F32R = mybir.dt.float32r
BF16 = mybir.dt.bfloat16
ALU = mybir.AluOpType
ACT = mybir.ActivationFunctionType
AX_X = mybir.AxisListType.X

WINDOW = 64
SINK = 4
HD = 64
LN_EPS = 1e-5
MASKED = -1.0e30
TINY = 1.1754943508222875e-38
BIG = 3.0e38


def layer_kernel(nc, X, Wq, Wk, Wv, Wo, ln1_g, ln1_b, w1, b1, ln2_g, ln2_b, w2, b2, out):
    B, T, D = X.shape
    NH = Wq.shape[1] // HD
    NKV = Wk.shape[1] // HD
    REP = NH // NKV
    HID = w1.shape[0]
    NQ = T // P
    KD = D // P
    KF = HID // P
    KO = NH * HD // P
    KM = NKV * HD // P
    HALO = WINDOW + SINK
    KEYS = P + HALO
    EXT = NQ * KEYS
    HALF = EXT // 2
    UNITS = NQ * NKV
    SCALE = 1.0 / HD ** 0.5
    assert T % P == 0 and REP == 4 and NQ == 4 and KD == 2 and P == 2 * WINDOW

    x_tiles = X.rearrange("b (n p) d -> p (b n) d", p=P)
    out_tiles = out.rearrange("b (n p) d -> p (b n) d", p=P)

    ctx = ExitStack()
    with ctx:
        def sb(name, shape, dt=F32, scope=ctx):
            return scope.enter_context(nc.sbuf_tensor(name, shape, dt))

        def sem(name):
            return ctx.enter_context(nc.semaphore(name))

        x_all = sb("x_all", [P, B * NQ, D])
        wq_hi, wq_lo = (sb(f"wq_{s}", [P, KD, NH * HD], F32R) for s in ("hi", "lo"))
        wk_hi, wk_lo = (sb(f"wk_{s}", [P, KD, NKV * HD], F32R) for s in ("hi", "lo"))
        wv_hi, wv_lo = (sb(f"wv_{s}", [P, KD, NKV * HD], F32R) for s in ("hi", "lo"))
        wo_hi, wo_lo = (sb(f"wo_{s}", [P, KO, D], F32R) for s in ("hi", "lo"))
        t1T = sb("t1T", [P, KD, HID], F32R)
        t2T = sb("t2T", [P, KF, D], F32R)
        bias1 = sb("bias1", [P, HID])
        bias2 = sb("bias2", [P, D])
        g1 = sb("g1", [P, KD])
        g2 = sb("g2", [P, KF])
        lnb1 = sb("lnb1", [P, KD])
        lnb2 = sb("lnb2", [P, KF])
        mask_first = sb("mask_first", [P, P])
        mask_rest = sb("mask_rest", [P, KEYS])
        ident = sb("ident", [P, P])
        ident_bf = sb("ident_bf", [P, P], BF16)
        ones = sb("ones", [P, P])
        neg_half = sb("neg_half", [P, NQ])
        wscale = sb("wscale", [P, 2])
        winv = sb("winv", [P, 2])
        gate = sb("gate", [P, 32])
        wsum = sb("wsum", [P, 2])
        wmean = sb("wmean", [P, 2])

        setup = ExitStack()
        with setup:
            st_wq = sb("st_wq", [P, KD, NH * HD], scope=setup)
            st_wk = sb("st_wk", [P, KD, NKV * HD], scope=setup)
            st_wv = sb("st_wv", [P, KD, NKV * HD], scope=setup)
            st_wo = sb("st_wo", [P, KO, D], scope=setup)
            st_w1 = sb("st_w1", [P, KF, D], scope=setup)
            st_w2 = sb("st_w2", [P, KD, HID], scope=setup)
            abs_w = sb("abs_w", [P, 2, KF * D], scope=setup)
            abs_64 = sb("abs_64", [P, 2, 64], scope=setup)
            abs_8 = sb("abs_8", [P, 2, 8], scope=setup)
            tot_row = sb("tot_row", [2, 8], scope=setup)
            tot = sb("tot", [2, 1], scope=setup)
            tot_diag = sb("tot_diag", [2, 2], scope=setup)
            pos = sb("pos", [P, KF * D], BF16, scope=setup)
            neg = sb("neg", [P, KF * D], BF16, scope=setup)
            tern = sb("tern", [P, 2, KF * D], BF16, scope=setup)

        attn = ExitStack()
        with attn:
            stats = sb("stats", [P, NQ, 6], scope=attn)
            moments = sb("moments", [P, NQ, 2], scope=attn)
            var_eps = sb("var_eps", [P, NQ], scope=attn)
            rstd = sb("rstd", [P, NQ], scope=attn)
            xt_hi, xt_lo = (sb(f"xt_{s}", [P, KD, NQ, KEYS], F32R, attn) for s in ("hi", "lo"))
            q_hi, q_lo = (sb(f"q_{s}", [P, KO, T], F32R, attn) for s in ("hi", "lo"))
            k_hi, k_lo = (sb(f"k_{s}", [P, KM, EXT], F32R, attn) for s in ("hi", "lo"))
            ks_hi, ks_lo = (sb(f"ks_{s}", [P, KM, EXT], F32R, attn) for s in ("hi", "lo"))
            v_own = sb("v_own", [P, NQ, NKV, 2, HD], scope=attn)
            v_halo = sb("v_halo", [HALO, NQ - 1, NKV, 2, HD], scope=attn)
            scores = sb("scores", [P, 2, REP, KEYS], scope=attn)
            xn = scores[:, :, :, :].rearrange("p a j k -> p (a j k)")[:, 0:NQ * D]\
                .rearrange("p (n d) -> p n d", n=NQ)
            probs = sb("probs", [P, 2, REP, KEYS], scope=attn)
            neg_max = sb("neg_max", [P, 2, REP], scope=attn)
            row_sum = sb("row_sum", [P, 2, REP], scope=attn)
            row_rec = sb("row_rec", [P, 2, REP], scope=attn)
            pt_own = sb("pt_own", [P, 2, REP * P], scope=attn)
            pt_halo = sb("pt_halo", [HALO, 2, REP * P], scope=attn)
            y_hi, y_lo = (sb(f"y_{s}", [P, KO, P], F32R, attn) for s in ("hi", "lo"))

        ffn = ExitStack()
        with ffn:
            f_stats = sb("f_stats", [P, NQ, 6], scope=ffn)
            f_moments = sb("f_moments", [P, NQ, 2], scope=ffn)
            f_var = sb("f_var", [P, NQ], scope=ffn)
            f_r1 = sb("f_r1", [P, NQ], scope=ffn)
            f_var2 = sb("f_var2", [P, NQ], scope=ffn)
            f_r2 = sb("f_r2", [P, NQ], scope=ffn)
            f_rstd = sb("f_rstd", [P, NQ], scope=ffn)
            f_xn = sb("f_xn", [P, NQ, D], scope=ffn)
            f_xb = sb("f_xb", [P, NQ, D], scope=ffn)
            f_out = sb("f_out", [P, NQ, D], scope=ffn)
            fx_hi, fx_lo = (sb(f"fx_{s}", [P, KD, T], F32R, ffn) for s in ("hi", "lo"))
            hid = sb("hid", [P, NQ, HID], scope=ffn)
            h_stats = sb("h_stats", [P, NQ, 2, 6], scope=ffn)
            h_moments = sb("h_moments", [P, NQ, 2], scope=ffn)
            h_var = sb("h_var", [P, NQ], scope=ffn)
            h_rstd = sb("h_rstd", [P, NQ], scope=ffn)
            ht_hi, ht_lo = (sb(f"ht_{s}", [P, KF, T], F32R, ffn) for s in ("hi", "lo"))

        psum = ExitStack()
        with psum:
            ps_score = [psum.enter_context(nc.psum_tensor(f"ps_score{i}", [P, 512], F32)) for i in range(2)]
            ps_job = [psum.enter_context(nc.psum_tensor(f"ps_job{i}", [P, 512], F32)) for i in range(2)]
            ps_pt_own = psum.enter_context(nc.psum_tensor("ps_pt_own", [P, 512], F32))
            ps_pt_halo = psum.enter_context(nc.psum_tensor("ps_pt_halo", [P, 512], F32))
            ps_y = [psum.enter_context(nc.psum_tensor(f"ps_y{i}", [P, 512], F32)) for i in range(2)]
        psum_ffn = ExitStack()
        with psum_ffn:
            ps_z = [psum_ffn.enter_context(nc.psum_tensor(f"ps_z{i}", [P, 1024], F32)) for i in range(2)]
            ps_t = [psum_ffn.enter_context(nc.psum_tensor(f"ps_t{i}", [P, 512], F32)) for i in range(2)]
            ps_o = [psum_ffn.enter_context(nc.psum_tensor(f"ps_o{i}", [P, 512], F32)) for i in range(2)]

        x_loaded = sem("x_loaded")
        w_loaded = [sem(f"w_loaded{i}") for i in range(4)]
        pool_consts = sem("pool_consts")
        masks_ready = sem("masks_ready")
        hi_ready = sem("hi_ready")
        abs_ready = sem("abs_ready")
        sums_ready = sem("sums_ready")
        total_ready = sem("total_ready")
        dve_step = sem("dve_step")
        tern_ready = sem("tern_ready")
        tern_T = sem("tern_T")
        tT_ready = sem("tT_ready")
        bias_mm = sem("bias_mm")
        setup_done = sem("setup_done")

        dve_chain = sem("dve_chain")
        var_ready = sem("var_ready")
        rstd_ready = sem("rstd_ready")
        xn_ready = sem("xn_ready")
        job_mm = sem("job_mm")
        job_hi = sem("job_hi")
        job_free = sem("job_free")
        ext_ready = sem("ext_ready")
        k_swapped = sem("k_swapped")
        score_mm = sem("score_mm")
        score_free = sem("score_free")
        exp_done = sem("exp_done")
        rec_chain = sem("rec_chain")
        rec_ready = sem("rec_ready")
        probs_ready = sem("probs_ready")
        pt_mm = sem("pt_mm")
        pt_own_done = sem("pt_own_done")
        pt_halo_done = sem("pt_halo_done")
        y_mm = sem("y_mm")
        y_hi_done = sem("y_hi_done")
        y_free = sem("y_free")

        f_chain = sem("f_chain")
        f_pow_in = sem("f_pow_in")
        f_pow_out = sem("f_pow_out")
        f_pool = sem("f_pool")
        f_xn_ready = sem("f_xn_ready")
        t_mm = sem("t_mm")
        t_hi = sem("t_hi")
        t_free = sem("t_free")
        z_mm = sem("z_mm")
        z_free = sem("z_free")
        gelu_done = sem("gelu_done")
        hn_ready = sem("hn_ready")
        o_mm = sem("o_mm")
        o_free = sem("o_free")
        stored = sem("stored")

        JOBS = KD + 2 * KM + NQ + KO + NQ
        J_K, J_V = KD, KD + 2 * KM
        J_Q = J_V + NQ
        J_O = J_Q + KO
        assert JOBS % 2 == 0
        T_JOBS = KD + KF
        assert T_JOBS % 2 == 0
        PAIRS = 2 * UNITS
        HALOS = UNITS - NKV

        block = ctx.enter_context(nc.Block())

        @block.sync
        def _(sp):
            sp.dma_start(st_w1[:, :, :], w1.rearrange("(n p) d -> p n d", p=P)).then_inc(w_loaded[1], 16)
            sp.dma_start(st_w2[:, :, :], w2.rearrange("(n p) h -> p n h", p=P)).then_inc(w_loaded[2], 16)
            with nc.allow_non_contiguous_dma(reason="per-partition vectors of the layer norms"):
                sp.dma_start(g1[:, :], ln1_g.rearrange("(k p) -> p k", p=P)).then_inc(w_loaded[3], 16)
                sp.dma_start(lnb1[:, :], ln1_b.rearrange("(k p) -> p k", p=P)).then_inc(w_loaded[3], 16)
                sp.dma_start(g2[:, :], ln2_g.rearrange("(k p) -> p k", p=P)).then_inc(w_loaded[3], 16)
                sp.dma_start(lnb2[:, :], ln2_b.rearrange("(k p) -> p k", p=P)).then_inc(w_loaded[3], 16)
            sp.dma_start(bias1[:, :], b1.partition_broadcast(P)).then_inc(w_loaded[3], 16)
            sp.dma_start(bias2[:, :], b2.partition_broadcast(P)).then_inc(w_loaded[3], 16)
            with sp.Fori(0, B) as b:
                sp.wait_ge(x_loaded, b * 16 + 16)
                sp.dma_start(x_all[:, bass.ds(b * NQ, NQ), :], x_tiles[:, bass.ds(b * NQ, NQ), :])\
                  .then_inc(x_loaded, 16)
            with sp.Fori(0, B) as b:
                sp.wait_ge(job_free, b * JOBS + (2 + J_V))
                for src, dst in ((k_hi, ks_hi), (k_lo, ks_lo)):
                    sp.dma_start(dst[0:HD, :, :].bitcast(F32), src[HD:P, :, :].bitcast(F32)).then_inc(k_swapped, 16)
                    sp.dma_start(dst[HD:P, :, :].bitcast(F32), src[0:HD, :, :].bitcast(F32)).then_inc(k_swapped, 16)
            with sp.Fori(0, B) as c:
                sp.wait_ge(o_free, c * NQ + (2 + NQ))
                sp.dma_start(out_tiles[:, bass.ds(c * NQ, NQ), :], f_out[:, :, :]).then_inc(stored, 16)
            sp.wait_ge(stored, 16 + 16 * B)

        @block.gpsimd
        def _(pool):
            def pool_gate():
                pool.tensor_tensor(gate[:, 0:1], ones[:, 0:1], ones[:, 0:1], ALU.mult)

            n = [0]

            def link(ins):
                n[0] += 1
                ins.then_inc(pool_consts, 1)
                pool.wait_ge(pool_consts, n[0])

            pool.memset(ones[:, :], 1.0)
            pool.memset(neg_half[:, :], -0.5)
            for m in (ident, ident_bf):
                link(pool.memset(m[:, :], 0.0))
                link(pool.affine_select(out=m[:, :], in_=m[:, :], compare_op=ALU.not_equal, fill=1.0,
                                        base=0, pattern=[[-1, P]], channel_multiplier=1))
            for m in (mask_first, mask_rest):
                link(pool.memset(m[:, :], 0.0))
                link(pool.affine_select(out=m[:, 0:P], in_=m[:, 0:P], compare_op=ALU.is_ge, fill=MASKED,
                                        base=0, pattern=[[-1, P]], channel_multiplier=1))
                lo = SINK if m is mask_first else 0
                link(pool.affine_select(out=m[:, lo:P], in_=m[:, lo:P], compare_op=ALU.is_ge, fill=MASKED,
                                        base=lo + WINDOW - 1, pattern=[[1, P - lo]], channel_multiplier=-1))
            link(pool.affine_select(out=mask_rest[:, P:P + WINDOW], in_=mask_rest[:, P:P + WINDOW],
                                    compare_op=ALU.is_ge, fill=MASKED, base=-1, pattern=[[1, WINDOW]],
                                    channel_multiplier=-1))
            pool.memset(gate[:, 31:32], 0.0).then_inc(masks_ready, 1)
            pool.wait_ge(setup_done, 1)
            for xt in (xt_hi, xt_lo):
                for k in range(KD):
                    pool.memset(xt[:, k, 0, P:KEYS].bitcast(F32), 0.0)

            with pool.Fori(0, B) as b:
                pool.wait_ge(var_ready, b + 1)
                pool.tensor_tensor(rstd[:, :], var_eps[:, :], neg_half[:, :], ALU.pow).then_inc(rstd_ready, 1)
                pool.wait_ge(job_free, b * JOBS + (2 + KD))
                pool_gate()
                for k in range(KD):
                    for xt in (xt_hi, xt_lo):
                        pool.tensor_copy(xt[:, k, 1:NQ, P:P + WINDOW], xt[:, k, 0:NQ - 1, WINDOW:P])
                        last = pool.tensor_copy(xt[:, k, 1:NQ, P + WINDOW:KEYS],
                                                xt[:, k, 0:1, 0:SINK].to_broadcast([P, NQ - 1, SINK]))
                last.then_inc(ext_ready, 1)
                for u in range(UNITS):
                    w = P if u < NKV else KEYS
                    pool.wait_ge(rec_ready, b * UNITS + (2 + u + 1))
                    pool.tensor_tensor(probs[:, u % 2, :, 0:w], probs[:, u % 2, :, 0:w],
                                       row_rec[:, u % 2, :].unsqueeze(2).to_broadcast([P, REP, w]), ALU.mult)\
                        .then_inc(probs_ready, 1)

            with pool.Fori(0, B) as c:
                pool.wait_ge(f_pow_in, c * (2 + NQ) + 1)
                pool.tensor_tensor(f_r1[:, :], f_var[:, :], neg_half[:, :], ALU.pow).then_inc(f_pow_out, 1)
                pool.wait_ge(f_pow_in, c * (2 + NQ) + 2)
                pool.tensor_tensor(f_r2[:, :], f_var2[:, :], neg_half[:, :], ALU.pow).then_inc(f_pow_out, 1)
                pool.wait_ge(o_free, c * NQ + 2)
                pool.tensor_tensor(f_xb[:, :, :], x_all[:, bass.ds(c * NQ, NQ), :],
                                   bias2[:, :].unsqueeze(1).to_broadcast([P, NQ, D]), ALU.add)\
                    .then_inc(f_pool, 1)
                for t in range(NQ):
                    pool.wait_ge(f_pow_in, c * (2 + NQ) + (3 + t))
                    pool.tensor_tensor(h_rstd[:, t:t + 1], h_var[:, t:t + 1], neg_half[:, 0:1], ALU.pow)\
                        .then_inc(f_pow_out, 1)
                    pool.wait_ge(f_pow_out, c * (2 + NQ) + (3 + t))
                    pool_gate()
                    pool.tensor_scalar(hid[:, t, :], hid[:, t, :], h_moments[:, t, 0:1], h_rstd[:, t:t + 1],
                                       ALU.subtract, ALU.mult).then_inc(hn_ready, 1)

        @block.scalar
        def _(act):
            for dst, src in ((st_wq, Wq), (st_wk, Wk), (st_wv, Wv), (st_wo, Wo)):
                act.dma_start(dst[:, :, :], src.rearrange("(k p) n -> p k n", p=P)).then_inc(w_loaded[0], 16)
            act.wait_ge(w_loaded[1], 16)
            act.activation(abs_w[:, 0, :], st_w1[:, :, :].rearrange("p n d -> p (n d)"), ACT.Abs).then_inc(abs_ready, 1)
            act.wait_ge(w_loaded[2], 16)
            act.activation(abs_w[:, 1, :], st_w2[:, :, :].rearrange("p n d -> p (n d)"), ACT.Abs).then_inc(abs_ready, 1)
            act.wait_ge(w_loaded[0], 64)
            for hi, src in ((wq_hi, st_wq), (wk_hi, st_wk), (wv_hi, st_wv), (wo_hi, st_wo)):
                act.activation(hi[:, :, :], src[:, :, :], ACT.Copy).then_inc(hi_ready, 1)
            act.wait_ge(setup_done, 1)

            def hi_part(b, job, dst, src, scale=1.0):
                act.wait_ge(job_mm, b * JOBS + (job + 1))
                act.activation(dst, src, ACT.Copy, scale=scale).then_inc(job_hi, 1)

            def exps(b, u):
                w = P if u < NKV else KEYS
                act.wait_ge(score_free, b * PAIRS + (2 + 2 * u + 2))
                act.wait_ge(rec_ready, b * UNITS + (u + 1))
                act.wait_ge(pt_mm, b * UNITS + (u + 1))
                for j in range(REP):
                    last = act.activation(probs[:, u % 2, j, 0:w], scores[:, u % 2, j, 0:w], ACT.Exp,
                                          bias=neg_max[:, u % 2, j:j + 1], scale=-1.0,
                                          accum_out=row_sum[:, u % 2, j:j + 1])
                last.then_inc(exp_done, 1)

            def copy_pt(b, u):
                act.wait_ge(pt_mm, b * UNITS + (2 + u + 1))
                act.wait_ge(y_mm, b * UNITS + (u + 1))
                act.activation(pt_own[:, u % 2, :], ps_pt_own[:, :], ACT.Copy).then_inc(pt_own_done, 1)

            def y_hi_part(b, u):
                qb, g = divmod(u, NKV)
                act.wait_ge(y_mm, b * UNITS + (2 + u + 1))
                if g == 0:
                    act.wait_ge(job_mm, b * JOBS + (J_O + qb))
                for half in range(2):
                    rows = slice(half * HD, (half + 1) * HD)
                    src = ps_y[u % 2][rows, :].rearrange("p (m h q) -> p m h q", m=2, h=2)[:, :, half, :]
                    last = act.activation(y_hi[rows, 2 * g:2 * g + 2, :], src, ACT.Copy)
                last.then_inc(y_hi_done, 1)

            with act.Fori(0, B) as b:
                for k in range(KD):
                    hi_part(b, k, xt_hi[:, k, :, 0:P], ps_job[k % 2][:, :].rearrange("p (n t) -> p n t", n=NQ))
                for i in range(2 * KM):
                    m, h = divmod(i, 2)
                    hi_part(b, J_K + i, k_hi[:, m, h * HALF:(h + 1) * HALF], ps_job[(J_K + i) % 2][:, 0:HALF])
                for m in range(KO):
                    hi_part(b, J_Q + m, q_hi[:, m, :], ps_job[(J_Q + m) % 2][:, :], scale=SCALE)
                for s in range(UNITS + 3):
                    if s < UNITS:
                        exps(b, s)
                    if 0 <= s - 2 < UNITS:
                        copy_pt(b, s - 2)
                    if 0 <= s - 3 < UNITS:
                        y_hi_part(b, s - 3)

            act.wait_ge(job_free, 2 + B * JOBS)
            with act.Fori(0, B) as c:
                def t_hi_part(job, dst, gain):
                    act.wait_ge(t_mm, c * T_JOBS + (job + 1))
                    act.activation(dst, ps_t[job % 2][:, :], ACT.Copy, scale=gain).then_inc(t_hi, 1)

                for k in range(KD):
                    t_hi_part(k, fx_hi[:, k, :], g1[:, k:k + 1])
                for t in range(NQ):
                    act.wait_ge(z_free, c * NQ + (2 + t + 1))
                    act.activation(hid[:, t, :], hid[:, t, :], ACT.Gelu).then_inc(gelu_done, 1)
                for k in range(KF):
                    t_hi_part(KD + k, ht_hi[:, k, :], g2[:, k:k + 1])

        @block.vector
        def _(dve):
            def dve_gate(i=0):
                dve.memset(gate[:, 1 + i:2 + i], 0.0)

            for i, (s, n) in enumerate(((job_free, 2), (score_free, 2), (exp_done, 2), (rec_ready, 2), (probs_ready, 2),
                         (pt_mm, 2), (pt_own_done, 1), (pt_halo_done, 1), (y_mm, 2), (y_free, 2),
                         (t_free, 2), (z_free, 2), (o_free, 2), (x_loaded, 16), (stored, 16))):
                dve.memset(gate[:, 8 + i:9 + i], 0.0).then_inc(s, n)
            steps = [0]

            def link(ins):
                steps[0] += 1
                ins.then_inc(dve_step, 1)
                dve.wait_ge(dve_step, steps[0])

            dve.wait_ge(masks_ready, 1)
            dve.wait_ge(abs_ready, 2)
            link(dve.tensor_reduce(abs_64[:, :, :], abs_w[:, :, :].rearrange("p w (a c) -> p w a c", a=64), AX_X, ALU.add))
            link(dve.tensor_reduce(abs_8[:, :, :], abs_64[:, :, :].rearrange("p w (a c) -> p w a c", a=8), AX_X, ALU.add))
            dve.tensor_reduce(wsum[:, :], abs_8[:, :, :], AX_X, ALU.add).then_inc(sums_ready, 1)
            dve.wait_ge(total_ready, 1)
            link(dve.tensor_reduce(tot_row[:, :], ps_job[0][0:2, 0:P].rearrange("w (a c) -> w a c", a=8), AX_X, ALU.add))
            link(dve.tensor_reduce(tot[:, :], tot_row[:, :], AX_X, ALU.add))
            dve.tensor_scalar(tot_diag[:, :], ident[0:2, 0:2], tot[:, 0:1], None, ALU.mult).then_inc(sums_ready, 1)
            dve.wait_ge(total_ready, 2)
            link(dve.tensor_scalar(wmean[:, :], ps_job[0][:, 0:2], 1.0 / (HID * D), 1e-5, ALU.mult, ALU.max))
            link(dve.reciprocal(wscale[:, :], wmean[:, :]))
            link(dve.reciprocal(winv[:, :], wscale[:, :]))
            for i, st in enumerate((st_w1, st_w2)):
                flat = st[:, :, :].rearrange("p n d -> p (n d)")
                link(dve.tensor_scalar(pos[:, :], flat, wscale[:, i:i + 1], 0.5, ALU.mult, ALU.is_gt))
                link(dve.tensor_scalar(neg[:, :], flat, wscale[:, i:i + 1], -0.5, ALU.mult, ALU.is_lt))
                dve.tensor_tensor(tern[:, i, :], pos[:, :], neg[:, :], ALU.subtract).then_inc(tern_ready, 1)
                dve.wait_ge(tern_ready, i + 1)
            for i, (lo, hi, src) in enumerate(((wq_lo, wq_hi, st_wq), (wk_lo, wk_hi, st_wk),
                                               (wv_lo, wv_hi, st_wv), (wo_lo, wo_hi, st_wo))):
                dve.wait_ge(hi_ready, i + 1)
                last = dve.tensor_tensor(lo[:, :, :], src[:, :, :], hi[:, :, :].bitcast(F32), ALU.subtract)
            for i, dst in enumerate((t1T[:, 0, :], t1T[:, 1, :],
                                     t2T[:, 0:KF // 2, :].rearrange("p k d -> p (k d)"),
                                     t2T[:, KF // 2:KF, :].rearrange("p k d -> p (k d)"))):
                dve.wait_ge(tern_T, i + 1)
                dve.tensor_copy(dst, (ps_score + ps_y)[i][:, :].bitcast(BF16)).then_inc(tT_ready, 1)
            dve.wait_ge(w_loaded[3], 96)
            dve.wait_ge(bias_mm, 1)
            for h in range(2):
                dve.scalar_tensor_tensor(out=bias1[:, 512 * h:512 * h + 512], in0=(ps_pt_own, ps_pt_halo)[h][:, :],
                                         scalar=winv[:, 0:1], in1=bias1[:, 512 * h:512 * h + 512],
                                         op0=ALU.mult, op1=ALU.add)
            dve.scalar_tensor_tensor(out=bias2[:, :], in0=ps_job[1][:, 0:D], scalar=winv[:, 1:2],
                                     in1=bias2[:, :], op0=ALU.mult, op1=ALU.add).then_inc(setup_done, 1)

            def lo_part(b, job, hi_index, dst, hi, src, scale=None):
                dve.wait_ge(job_hi, b * (KD + 2 * KM + KO) + (hi_index + 1))
                if scale is None:
                    ins = dve.tensor_tensor(dst, src, hi.bitcast(F32), ALU.subtract)
                else:
                    ins = dve.scalar_tensor_tensor(out=dst, in0=src, scalar=scale, in1=hi.bitcast(F32),
                                                   op0=ALU.mult, op1=ALU.subtract)
                ins.then_inc(job_free, 1)

            def mask_and_max(b, u):
                w = P if u < NKV else KEYS
                mask = mask_first if u < NKV else mask_rest
                dve.wait_ge(exp_done, b * UNITS + (u + 1))
                for pair in range(2):
                    dve.wait_ge(score_mm, b * PAIRS + (2 * u + pair + 1))
                    dve_gate(1 + (2 * u + pair) % 4)
                    for j in (pair, pair + 2):
                        last = dve.tensor_tensor_reduce(
                            scores[:, u % 2, j, 0:w], ps_score[pair][:, (j // 2) * 256:(j // 2) * 256 + w],
                            mask[:, 0:w], -1.0, BIG, ALU.add, ALU.min, neg_max[:, u % 2, j:j + 1])
                    last.then_inc(score_free, 1)

            def reciprocals(b, u):
                dve.wait_ge(exp_done, b * UNITS + (2 + u + 1))
                dve.wait_ge(probs_ready, b * UNITS + (u + 1))
                dve.tensor_scalar(row_rec[:, u % 2, :], row_sum[:, u % 2, :], TINY, None, ALU.max)\
                    .then_inc(rec_chain, 1)
                dve.wait_ge(rec_chain, b * UNITS + (u + 1))
                dve.reciprocal(row_rec[:, u % 2, :], row_rec[:, u % 2, :]).then_inc(rec_ready, 1)

            def copy_pt(b, u):
                dve.wait_ge(pt_mm, b * UNITS + (2 + u + 1))
                dve.wait_ge(y_mm, b * UNITS + (u + 1))
                dve.tensor_copy(pt_halo[:, u % 2, :], ps_pt_halo[0:HALO, :]).then_inc(pt_halo_done, 1)

            def y_lo_part(b, u):
                g = u % NKV
                dve.wait_ge(y_hi_done, b * UNITS + (u + 1))
                for half in range(2):
                    rows = slice(half * HD, (half + 1) * HD)
                    src = ps_y[u % 2][rows, :].rearrange("p (m h q) -> p m h q", m=2, h=2)[:, :, half, :]
                    last = dve.tensor_tensor(y_lo[rows, 2 * g:2 * g + 2, :], src,
                                             y_hi[rows, 2 * g:2 * g + 2, :].bitcast(F32), ALU.subtract)
                last.then_inc(y_free, 1)

            def add_residual(b, qb):
                dve.wait_ge(job_mm, b * JOBS + (J_O + qb + 1))
                row = x_all[:, bass.ds(b * NQ + qb, 1), :].rearrange("p o d -> p (o d)")
                dve.tensor_tensor(row, row, ps_job[(J_O + qb) % 2][:, 0:D], ALU.add).then_inc(job_free, 1)

            CHAIN = 2
            with dve.Fori(0, B) as b:
                dve.wait_ge(x_loaded, b * 16 + 32)
                for n in range(NQ):
                    row = x_all[:, bass.ds(b * NQ + n, 1), :].rearrange("p o d -> p (o d)")
                    last = dve.bn_stats(stats[:, n, :], row)
                last.then_inc(dve_chain, 1)
                dve.wait_ge(dve_chain, b * CHAIN + 1)
                dve_gate()
                for n in range(NQ):
                    last = dve.bn_aggr(moments[:, n, :], stats[:, n, :])
                last.then_inc(dve_chain, 1)
                dve.wait_ge(dve_chain, b * CHAIN + 2)
                dve.tensor_scalar(var_eps[:, :], moments[:, :, 1], LN_EPS, None, ALU.add).then_inc(var_ready, 1)
                dve.wait_ge(rstd_ready, b + 1)
                for n in range(NQ):
                    row = x_all[:, bass.ds(b * NQ + n, 1), :].rearrange("p o d -> p (o d)")
                    last = dve.tensor_scalar(xn[:, n, :], row, moments[:, n, 0:1], rstd[:, n:n + 1],
                                             ALU.subtract, ALU.mult)
                last.then_inc(xn_ready, 1)
                for k in range(KD):
                    lo_part(b, k, k, xt_lo[:, k, :, 0:P], xt_hi[:, k, :, 0:P],
                            ps_job[k % 2][:, :].rearrange("p (n t) -> p n t", n=NQ))
                for i in range(2 * KM):
                    m, h = divmod(i, 2)
                    cols = slice(h * HALF, (h + 1) * HALF)
                    lo_part(b, J_K + i, KD + i, k_lo[:, m, cols], k_hi[:, m, cols],
                            ps_job[(J_K + i) % 2][:, 0:HALF])
                for n in range(NQ):
                    dve.wait_ge(job_mm, b * JOBS + (J_V + n + 1))
                    bank = ps_job[(J_V + n) % 2]
                    own = bank[:, 0:NKV * HD].rearrange("p (g o d) -> p g o d", g=NKV, o=1)
                    ins = dve.tensor_copy(v_own[:, n, :, :, :], own.to_broadcast([P, NKV, 2, HD]))
                    if n:
                        halo = bank[0:HALO, 256:256 + NKV * HD].rearrange("p (g o d) -> p g o d", g=NKV, o=1)
                        ins = dve.tensor_copy(v_halo[:, n - 1, :, :, :], halo.to_broadcast([HALO, NKV, 2, HD]))
                    ins.then_inc(job_free, 1)
                for m in range(KO):
                    lo_part(b, J_Q + m, KD + 2 * KM + m, q_lo[:, m, :], q_hi[:, m, :],
                            ps_job[(J_Q + m) % 2][:, :], scale=SCALE)
                for s in range(UNITS + 4):
                    if s < UNITS:
                        mask_and_max(b, s)
                    if 0 <= s - 1 < UNITS:
                        reciprocals(b, s - 1)
                    if NKV <= s - 2 < UNITS:
                        copy_pt(b, s - 2)
                    if 0 <= s - 3 < UNITS:
                        y_lo_part(b, s - 3)
                    if s >= 4 and (s - 4) % NKV == NKV - 1:
                        add_residual(b, (s - 4) // NKV)

            dve.wait_ge(job_free, 2 + B * JOBS)
            F_CHAIN = 5 + 2 * NQ

            with dve.Fori(0, B) as c:
                links = [0]

                def step(ins):
                    links[0] += 1
                    ins.then_inc(f_chain, 1)
                    dve.wait_ge(f_chain, c * F_CHAIN + links[0])
                    dve_gate()

                for n in range(NQ):
                    row = x_all[:, bass.ds(c * NQ + n, 1), :].rearrange("p o d -> p (o d)")
                    last = dve.bn_stats(f_stats[:, n, :], row)
                step(last)
                for n in range(NQ):
                    last = dve.bn_aggr(f_moments[:, n, :], f_stats[:, n, :])
                step(last)
                dve.tensor_scalar(f_var[:, :], f_moments[:, :, 1], LN_EPS, None, ALU.add).then_inc(f_pow_in, 1)
                dve.wait_ge(f_pow_out, c * (2 + NQ) + 1)
                step(dve.tensor_tensor(f_var2[:, :], f_moments[:, :, 1], f_r1[:, :], ALU.mult))
                step(dve.tensor_tensor(f_var2[:, :], f_var2[:, :], f_r1[:, :], ALU.mult))
                dve.tensor_scalar(f_var2[:, :], f_var2[:, :], LN_EPS, None, ALU.add).then_inc(f_pow_in, 1)
                dve.wait_ge(f_pow_out, c * (2 + NQ) + 2)
                step(dve.tensor_tensor(f_rstd[:, :], f_r1[:, :], f_r2[:, :], ALU.mult))
                for n in range(NQ):
                    row = x_all[:, bass.ds(c * NQ + n, 1), :].rearrange("p o d -> p (o d)")
                    last = dve.tensor_scalar(f_xn[:, n, :], row, f_moments[:, n, 0:1], f_rstd[:, n:n + 1],
                                             ALU.subtract, ALU.mult)
                last.then_inc(f_xn_ready, 1)

                def t_lo_part(job, dst, hi, gain):
                    dve.wait_ge(t_hi, c * T_JOBS + (job + 1))
                    dve.scalar_tensor_tensor(out=dst, in0=ps_t[job % 2][:, :], scalar=gain, in1=hi.bitcast(F32),
                                             op0=ALU.mult, op1=ALU.subtract).then_inc(t_free, 1)

                for k in range(KD):
                    t_lo_part(k, fx_lo[:, k, :], fx_hi[:, k, :], g1[:, k:k + 1])

                def hidden(t):
                    dve.wait_ge(z_mm, c * NQ + (t + 1))
                    dve.scalar_tensor_tensor(out=hid[:, t, :], in0=ps_z[t % 2][:, :], scalar=winv[:, 0:1],
                                             in1=bias1[:, :], op0=ALU.mult, op1=ALU.add).then_inc(z_free, 1)

                def hidden_stats(t):
                    dve.wait_ge(gelu_done, c * NQ + (t + 1))
                    dve.bn_stats(h_stats[:, t, 0, :], hid[:, t, 0:512])
                    step(dve.bn_stats(h_stats[:, t, 1, :], hid[:, t, 512:1024]))
                    step(dve.bn_aggr(h_moments[:, t, :], h_stats[:, t, :, :].rearrange("p a s -> p (a s)")))
                    dve.tensor_scalar(h_var[:, t:t + 1], h_moments[:, t, 1:2], LN_EPS, None, ALU.add)\
                        .then_inc(f_pow_in, 1)

                for t in range(NQ + 1):
                    if t < NQ:
                        hidden(t)
                    if t >= 1:
                        hidden_stats(t - 1)
                for k in range(KF):
                    t_lo_part(KD + k, ht_lo[:, k, :], ht_hi[:, k, :], g2[:, k:k + 1])
                dve.wait_ge(stored, c * 16 + 16)
                dve.wait_ge(f_pool, c + 1)
                for t in range(NQ):
                    dve.wait_ge(o_mm, c * NQ + (t + 1))
                    dve.scalar_tensor_tensor(out=f_out[:, t, :], in0=ps_o[t % 2][:, 0:D], scalar=winv[:, 1:2],
                                             in1=f_xb[:, t, :], op0=ALU.mult, op1=ALU.add).then_inc(o_free, 1)
                assert links[0] == F_CHAIN

        @block.tensor
        def _(pe):
            pe.wait_ge(masks_ready, 1)
            pe.wait_ge(sums_ready, 1)
            pe.transpose(ps_job[0][0:2, 0:P], wsum[:, :], ident[:, :]).then_inc(total_ready, 1)
            pe.wait_ge(sums_ready, 2)
            pe.matmul(ps_job[0][:, 0:2], ones[0:2, :], tot_diag[:, :], start=True, stop=True).then_inc(total_ready, 1)
            for i in range(4):
                bank = (ps_score + ps_y)[i][:, :].bitcast(BF16)
                pe.wait_ge(tern_ready, i // 2 + 1)
                for n in range(KF):
                    if i < 2:
                        src = tern[:, 0, n * D + i * P:n * D + (i + 1) * P]
                    else:
                        k, d = (i - 2) * (KF // 2) + n // 2, n % 2
                        src = tern[:, 1, d * HID + k * P:d * HID + (k + 1) * P]
                    last = pe.transpose(bank[:, n * P:(n + 1) * P], src, ident_bf[:, :])
                last.then_inc(tern_T, 1)
            pe.wait_ge(tT_ready, 4)
            pe.wait_ge(w_loaded[3], 96)
            for h in range(2):
                for k in range(KD):
                    pe.matmul((ps_pt_own, ps_pt_halo)[h][:, :], lnb1[:, k:k + 1].to_broadcast([P, P]),
                              t1T[:, k, 512 * h:512 * h + 512].bitcast(F32), start=(k == 0), stop=(k == KD - 1))
            for k in range(KF):
                last = pe.matmul(ps_job[1][:, 0:D], lnb2[:, k:k + 1].to_broadcast([P, P]),
                                 t2T[:, k, :].bitcast(F32), start=(k == 0), stop=(k == KF - 1))
            last.then_inc(bias_mm, 1)
            pe.wait_ge(setup_done, 1)

            def split_matmul(dst, terms):
                n = len(terms)
                for i, (s_hi, s_lo, m_hi, m_lo) in enumerate(terms):
                    pe.matmul(dst, s_hi, m_hi, start=(i == 0), stop=False)
                    pe.matmul(dst, s_hi, m_lo, start=False, stop=False)
                    last = pe.matmul(dst, s_lo, m_hi, start=False, stop=(i == n - 1))
                return last

            def scores_of(b, u, pair):
                qb, g = divmod(u, NKV)
                w = P if qb == 0 else KEYS
                pe.wait_ge(score_free, b * PAIRS + (2 * u + pair + 1))
                half = pair
                for j in (pair, pair + 2):
                    rows = slice(half * HD, (half + 1) * HD)
                    kh, kl = (k_hi, k_lo) if g % 2 == half else (ks_hi, ks_lo)
                    m = (REP * g + j) // 2
                    last = split_matmul(ps_score[pair][:, (j // 2) * 256:(j // 2) * 256 + w],
                                        [(q_hi[rows, m, qb * P:(qb + 1) * P], q_lo[rows, m, qb * P:(qb + 1) * P],
                                          kh[rows, g // 2, qb * KEYS:qb * KEYS + w],
                                          kl[rows, g // 2, qb * KEYS:qb * KEYS + w])])
                last.then_inc(score_mm, 1)

            def transpose_probs(b, u):
                pe.wait_ge(probs_ready, b * UNITS + (2 + u + 1))
                pe.wait_ge(pt_own_done, b * UNITS + (u + 1))
                if u >= NKV:
                    pe.wait_ge(pt_halo_done, b * HALOS + (u - NKV + 1))
                for j in range(REP):
                    last = pe.transpose(ps_pt_own[:, j * P:(j + 1) * P], probs[:, u % 2, j, 0:P], ident[:, :])
                if u >= NKV:
                    for j in range(REP):
                        last = pe.transpose(ps_pt_halo[0:HALO, j * P:(j + 1) * P], probs[:, u % 2, j, P:KEYS],
                                            ident[:, :])
                last.then_inc(pt_mm, 1)

            def outputs_of(b, u):
                qb, g = divmod(u, NKV)
                pe.wait_ge(pt_own_done, b * UNITS + (1 + u + 1))
                if qb:
                    pe.wait_ge(pt_halo_done, b * HALOS + (1 + u - NKV + 1))
                pe.wait_ge(y_free, b * UNITS + (u + 1))
                v = v_own[:, qb, g, :, :].rearrange("p t d -> p (t d)")
                last = pe.matmul(ps_y[u % 2][:, :], v, pt_own[:, u % 2, :], start=True, stop=(qb == 0))
                if qb:
                    v = v_halo[:, qb - 1, g, :, :].rearrange("p t d -> p (t d)")
                    last = pe.matmul(ps_y[u % 2][:, :], v, pt_halo[:, u % 2, :], start=False, stop=True)
                last.then_inc(y_mm, 1)

            def output_product(b, qb):
                pe.wait_ge(y_free, b * UNITS + (2 + (qb + 1) * NKV))
                pe.wait_ge(job_free, b * JOBS + (J_O + qb + 1))
                split_matmul(ps_job[(J_O + qb) % 2][:, 0:D],
                             [(y_hi[:, k, :], y_lo[:, k, :], wo_hi[:, k, :], wo_lo[:, k, :]) for k in range(KO)])\
                    .then_inc(job_mm, 1)

            with pe.Fori(0, B) as b:
                pe.wait_ge(xn_ready, b + 1)
                for k in range(KD):
                    pe.wait_ge(job_free, b * JOBS + (k + 1))
                    for n in range(NQ):
                        last = pe.transpose(ps_job[k % 2][:, n * P:(n + 1) * P], xn[:, n, k * P:(k + 1) * P],
                                            ident[:, :])
                    last.then_inc(job_mm, 1)
                pe.wait_ge(ext_ready, b + 1)
                for i in range(2 * KM):
                    m, h = divmod(i, 2)
                    pe.wait_ge(job_free, b * JOBS + (J_K + i + 1))
                    cols = slice(h * (NQ // 2), (h + 1) * (NQ // 2))
                    split_matmul(ps_job[(J_K + i) % 2][:, 0:HALF],
                                 [(wk_hi[:, k, m * P:(m + 1) * P], wk_lo[:, k, m * P:(m + 1) * P],
                                   xt_hi[:, k, cols, :], xt_lo[:, k, cols, :]) for k in range(KD)])\
                        .then_inc(job_mm, 1)
                for n in range(NQ):
                    pe.wait_ge(job_free, b * JOBS + (J_V + n + 1))
                    bank = ps_job[(J_V + n) % 2]
                    last = split_matmul(bank[:, 0:256],
                                        [(xt_hi[:, k, n, 0:P], xt_lo[:, k, n, 0:P], wv_hi[:, k, :], wv_lo[:, k, :])
                                         for k in range(KD)])
                    if n:
                        last = split_matmul(bank[0:HALO, 256:512],
                                            [(xt_hi[:, k, n, P:KEYS], xt_lo[:, k, n, P:KEYS],
                                              wv_hi[:, k, :], wv_lo[:, k, :]) for k in range(KD)])
                    last.then_inc(job_mm, 1)
                for m in range(KO):
                    pe.wait_ge(job_free, b * JOBS + (J_Q + m + 1))
                    split_matmul(ps_job[(J_Q + m) % 2][:, :],
                                 [(wq_hi[:, k, m * P:(m + 1) * P], wq_lo[:, k, m * P:(m + 1) * P],
                                   xt_hi[:, k, :, 0:P], xt_lo[:, k, :, 0:P]) for k in range(KD)])\
                        .then_inc(job_mm, 1)
                pe.wait_ge(job_free, b * JOBS + (2 + J_O))
                pe.wait_ge(k_swapped, b * 64 + 64)
                for s in range(UNITS + 4):
                    if s < UNITS:
                        scores_of(b, s, 0)
                    if 0 <= s - 2 < UNITS:
                        transpose_probs(b, s - 2)
                    if s < UNITS:
                        scores_of(b, s, 1)
                    if 0 <= s - 3 < UNITS:
                        outputs_of(b, s - 3)
                    if s >= 4 and (s - 4) % NKV == NKV - 1:
                        output_product(b, (s - 4) // NKV)

            def ternary_matmul(dst, terms):
                n = len(terms)
                for i, (a_hi, a_lo, w) in enumerate(terms):
                    pe.matmul(dst, a_hi, w, start=(i == 0), stop=False)
                    last = pe.matmul(dst, a_lo, w, start=False, stop=(i == n - 1))
                return last

            with pe.Fori(0, B) as c:
                pe.wait_ge(f_xn_ready, c + 1)
                for k in range(KD):
                    pe.wait_ge(t_free, c * T_JOBS + (k + 1))
                    for n in range(NQ):
                        last = pe.transpose(ps_t[k % 2][:, n * P:(n + 1) * P], f_xn[:, n, k * P:(k + 1) * P],
                                            ident[:, :])
                    last.then_inc(t_mm, 1)
                pe.wait_ge(t_free, c * T_JOBS + (2 + KD))
                for t in range(NQ):
                    pe.wait_ge(z_free, c * NQ + (t + 1))
                    for h in range(2):
                        last = ternary_matmul(ps_z[t % 2][:, 512 * h:512 * h + 512],
                                              [(fx_hi[:, k, t * P:(t + 1) * P], fx_lo[:, k, t * P:(t + 1) * P],
                                                t1T[:, k, 512 * h:512 * h + 512]) for k in range(KD)])
                    last.then_inc(z_mm, 1)
                pe.wait_ge(hn_ready, c * NQ + NQ)
                for k in range(KF):
                    pe.wait_ge(t_free, c * T_JOBS + (KD + k + 1))
                    for n in range(NQ):
                        last = pe.transpose(ps_t[(KD + k) % 2][:, n * P:(n + 1) * P],
                                            hid[:, n, k * P:(k + 1) * P], ident[:, :])
                    last.then_inc(t_mm, 1)
                pe.wait_ge(t_free, c * T_JOBS + (2 + T_JOBS))
                for t in range(NQ):
                    pe.wait_ge(o_free, c * NQ + (t + 1))
                    ternary_matmul(ps_o[t % 2][:, 0:D],
                                   [(ht_hi[:, k, t * P:(t + 1) * P], ht_lo[:, k, t * P:(t + 1) * P], t2T[:, k, :])
                                    for k in range(KF)]).then_inc(o_mm, 1)


_INS = ['L0_attn_X', 'L0_attn_Wq', 'L0_attn_Wk', 'L0_attn_Wv', 'L0_attn_Wo', 'L0_ffn_ln1_g', 'L0_ffn_ln1_b',
        'L0_ffn_w1', 'L0_ffn_b1', 'L0_ffn_ln2_g', 'L0_ffn_ln2_b', 'L0_ffn_w2', 'L0_ffn_b2']
_OUTS = [((8, 512, 256), 'float32')]


def kernel(**inputs):
    import numpy as _np
    import concourse.bacc as _bacc
    from concourse import mybir as _mybir
    from concourse.bass_utils import run_bass_kernel_spmd as _run

    nc = _bacc.Bacc("TRN2", target_bir_lowering=False, num_devices=1)
    arrays, args = {}, []
    for name in _INS:
        a = _np.ascontiguousarray(inputs[name])
        arrays[f"in_{name}_dram"] = a
        args.append(nc.dram_tensor(f"in_{name}_dram", a.shape, _mybir.dt.from_np(a.dtype), kind="ExternalInput").ap())
    for i, (shape, dtype) in enumerate(_OUTS):
        dt = _mybir.dt.from_np(_np.dtype(dtype))
        args.append(nc.dram_tensor(f"out_{i}_dram", shape, dt, kind="ExternalOutput").ap())
    layer_kernel(nc, *args)
    r = _run(nc, [arrays], core_ids=[0])
    return r.results[0]["out_0_dram"]
```

```python
from contextlib import ExitStack

import concourse.bass as bass
from concourse import mybir

P = 128
F32 = mybir.dt.float32
F32R = mybir.dt.float32r
BF16 = mybir.dt.bfloat16
ALU = mybir.AluOpType
ACT = mybir.ActivationFunctionType
AX_X = mybir.AxisListType.X

WINDOW = 64
SINK = 4
HD = 64
LN_EPS = 1e-5
MASKED = -1.0e30
TINY = 1.1754943508222875e-38
BIG = 3.0e38


def layer_kernel(nc, X, Wq, Wk, Wv, Wo, ln1_g, ln1_b, w1, b1, ln2_g, ln2_b, w2, b2, out):
    B, T, D = X.shape
    NH = Wq.shape[1] // HD
    NKV = Wk.shape[1] // HD
    REP = NH // NKV
    HID = w1.shape[0]
    NQ = T // P
    KD = D // P
    KF = HID // P
    KO = NH * HD // P
    KM = NKV * HD // P
    HALO = WINDOW + SINK
    KEYS = P + HALO
    EXT = NQ * KEYS
    HALF = EXT // 2
    UNITS = NQ * NKV
    NT = B * NQ
    SCALE = 1.0 / HD ** 0.5
    assert T % P == 0 and REP == 4 and NQ == 4 and KD == 2 and P == 2 * WINDOW

    x_tiles = X.rearrange("b (n p) d -> p (b n) d", p=P)
    out_tiles = out.rearrange("b (n p) d -> p (b n) d", p=P)

    ctx = ExitStack()
    with ctx:
        def sb(name, shape, dt=F32, scope=ctx):
            return scope.enter_context(nc.sbuf_tensor(name, shape, dt))

        def sem(name):
            return ctx.enter_context(nc.semaphore(name))

        x_all = sb("x_all", [P, B * NQ, D])
        wq_hi, wq_lo = (sb(f"wq_{s}", [P, KD, NH * HD], F32R) for s in ("hi", "lo"))
        wk_hi, wk_lo = (sb(f"wk_{s}", [P, KD, NKV * HD], F32R) for s in ("hi", "lo"))
        wv_hi, wv_lo = (sb(f"wv_{s}", [P, KD, NKV * HD], F32R) for s in ("hi", "lo"))
        wo_hi, wo_lo = (sb(f"wo_{s}", [P, KO, D], F32R) for s in ("hi", "lo"))
        t1T = sb("t1T", [P, KD, HID], F32R)
        t2T = sb("t2T", [P, KF, D], F32R)
        x_stats = sb("x_stats", [P, B * NQ, 6])
        lnb1 = sb("lnb1", [P, KD])
        lnb2 = sb("lnb2", [P, KF])
        mask_first = sb("mask_first", [P, P])
        mask_rest = sb("mask_rest", [P, KEYS])
        ident = sb("ident", [P, P])
        ident_bf = sb("ident_bf", [P, P], BF16)
        ones = sb("ones", [P, P])
        neg_half = sb("neg_half", [P, B * NQ])
        wscale = sb("wscale", [P, 2])
        winv = sb("winv", [P, 2])
        gate = sb("gate", [P, 32])
        wsum = sb("wsum", [P, 2])
        wmean = sb("wmean", [P, 2])
        wscale_sq = sb("wscale_sq", [P, 2])

        setup = ExitStack()
        with setup:
            st_wq = sb("st_wq", [P, KD, NH * HD], scope=setup)
            st_wk = sb("st_wk", [P, KD, NKV * HD], scope=setup)
            st_wv = sb("st_wv", [P, KD, NKV * HD], scope=setup)
            st_wo = sb("st_wo", [P, KO, D], scope=setup)
            st_w1 = sb("st_w1", [P, KF, D], scope=setup)
            st_w2 = sb("st_w2", [P, KD, HID], scope=setup)
            abs_w = sb("abs_w", [P, 2, KF * D], scope=setup)
            abs_64 = sb("abs_64", [P, 2, 64], scope=setup)
            abs_8 = sb("abs_8", [P, 2, 8], scope=setup)
            tot_row = sb("tot_row", [2, 8], scope=setup)
            tot = sb("tot", [2, 1], scope=setup)
            tot_diag = sb("tot_diag", [2, 2], scope=setup)
            pos = sb("pos", [P, KF * D], BF16, scope=setup)
            neg = sb("neg", [P, KF * D], BF16, scope=setup)
            tern = sb("tern", [P, 2, KF * D], BF16, scope=setup)

        attn = ExitStack()
        with attn:
            stats = sb("stats", [P, NQ, 6], scope=attn)
            moments = sb("moments", [P, NQ, 2], scope=attn)
            var_eps = sb("var_eps", [P, NQ], scope=attn)
            rstd = sb("rstd", [P, NQ], scope=attn)
            xt_hi, xt_lo = (sb(f"xt_{s}", [P, KD, NQ, KEYS], F32R, attn) for s in ("hi", "lo"))
            q_hi, q_lo = (sb(f"q_{s}", [P, 2, 2, T], F32R, attn) for s in ("hi", "lo"))
            k_hi, k_lo = (sb(f"k_{s}", [P, KM, EXT], F32R, attn) for s in ("hi", "lo"))
            ks_hi, ks_lo = (sb(f"ks_{s}", [P, KM, EXT], F32R, attn) for s in ("hi", "lo"))
            v_own = sb("v_own", [P, NQ, NKV, 2, HD], scope=attn)
            v_halo = sb("v_halo", [HALO, NQ - 1, NKV, 2, HD], scope=attn)
            scores = sb("scores", [P, 2, REP, KEYS], scope=attn)
            xn = sb("xn", [P, NQ, D], scope=attn)
            probs = sb("probs", [P, 4, REP, KEYS], scope=attn)
            neg_max = sb("neg_max", [P, 2, REP], scope=attn)
            row_sum = sb("row_sum", [P, 2, REP], scope=attn)
            row_rec = sb("row_rec", [P, 2, REP], scope=attn)
            pt_own = sb("pt_own", [P, 2, REP * P], scope=attn)
            pt_halo = sb("pt_halo", [HALO, 2, REP * P], scope=attn)
            y_hi, y_lo = (sb(f"y_{s}", [P, NQ, KO // 2, P], F32R, attn) for s in ("hi", "lo"))

        ffn = ExitStack()
        with ffn:
            bias1 = sb("bias1", [P, HID], scope=ffn)
            bias2 = sb("bias2", [P, D], scope=ffn)
            gain1 = sb("gain1", [P, D], scope=ffn)
            gain2 = sb("gain2", [P, HID], scope=ffn)
            f_moments = sb("f_moments", [P, NT, 2], scope=ffn)
            f_var = sb("f_var", [P, NT], scope=ffn)
            f_r1 = sb("f_r1", [P, NT], scope=ffn)
            f_var2 = sb("f_var2", [P, NT], scope=ffn)
            f_r2 = sb("f_r2", [P, NT], scope=ffn)
            scale1 = sb("scale1", [P, NT], scope=ffn)
            f_xm = sb("f_xm", [P, 2, D], scope=ffn)
            f_xb = sb("f_xb", [P, 4, D], scope=ffn)
            f_out = sb("f_out", [P, 4, D], scope=ffn)
            fx_hi, fx_lo = (sb(f"fx_{s}", [P, 2, D], F32R, ffn) for s in ("hi", "lo"))
            hid = sb("hid", [P, 4, HID], scope=ffn)
            h_stats = sb("h_stats", [P, 4, 2, 6], scope=ffn)
            h_moments = sb("h_moments", [P, 4, 2], scope=ffn)
            h_negmean = sb("h_negmean", [P, 4], scope=ffn)
            h_var = sb("h_var", [P, 4], scope=ffn)
            scale2 = sb("scale2", [P, 4], scope=ffn)
            ht_hi, ht_lo = (sb(f"ht_{s}", [P, HID], F32R, ffn) for s in ("hi", "lo"))

        psum = ExitStack()
        with psum:
            ps_score = [psum.enter_context(nc.psum_tensor(f"ps_score{i}", [P, 512], F32)) for i in range(2)]
            ps_job = [psum.enter_context(nc.psum_tensor(f"ps_job{i}", [P, 512], F32)) for i in range(2)]
            ps_pt_own = psum.enter_context(nc.psum_tensor("ps_pt_own", [P, 512], F32))
            ps_pt_halo = psum.enter_context(nc.psum_tensor("ps_pt_halo", [P, 512], F32))
            ps_y = [psum.enter_context(nc.psum_tensor(f"ps_y{i}", [P, 512], F32)) for i in range(2)]
        psum_ffn = ExitStack()
        with psum_ffn:
            ps_z = [psum_ffn.enter_context(nc.psum_tensor(f"ps_z{i}", [P, 1024], F32)) for i in range(2)]
            ps_th = [psum_ffn.enter_context(nc.psum_tensor(f"ps_th{i}", [P, 512], F32)) for i in range(2)]
            ps_tx = psum_ffn.enter_context(nc.psum_tensor("ps_tx", [P, 512], F32))
            ps_o = psum_ffn.enter_context(nc.psum_tensor("ps_o", [P, 512], F32))

        x_loaded = sem("x_loaded")
        w_loaded = [sem(f"w_loaded{i}") for i in range(4)]
        pool_consts = sem("pool_consts")
        masks_ready = sem("masks_ready")
        hi_ready = sem("hi_ready")
        abs_ready = sem("abs_ready")
        sums_ready = sem("sums_ready")
        total_ready = sem("total_ready")
        dve_step = sem("dve_step")
        tern_ready = sem("tern_ready")
        tern_T = sem("tern_T")
        tT_ready = sem("tT_ready")
        bias_mm = sem("bias_mm")
        setup_done = sem("setup_done")

        dve_chain = sem("dve_chain")
        var_ready = sem("var_ready")
        rstd_ready = sem("rstd_ready")
        xn_ready = sem("xn_ready")
        job_mm = sem("job_mm")
        job_hi = sem("job_hi")
        job_free = sem("job_free")
        ext_ready = sem("ext_ready")
        k_swapped = sem("k_swapped")
        score_mm = sem("score_mm")
        score_free = sem("score_free")
        exp_done = sem("exp_done")
        rec_chain = sem("rec_chain")
        rec_ready = sem("rec_ready")
        probs_ready = sem("probs_ready")
        pt_mm = sem("pt_mm")
        pt_own_done = sem("pt_own_done")
        pt_halo_done = sem("pt_halo_done")
        y_mm = sem("y_mm")
        y_hi_done = sem("y_hi_done")
        y_free = sem("y_free")

        ffn_loaded = sem("ffn_loaded")
        fbias_mm = sem("fbias_mm")
        f_chain = sem("f_chain")
        f_pow_in = sem("f_pow_in")
        f_pow_out = sem("f_pow_out")
        xm_ready = sem("xm_ready")
        xb_ready = sem("xb_ready")
        tx_mm = sem("tx_mm")
        tx_hi = sem("tx_hi")
        tx_free = sem("tx_free")
        z_mm = sem("z_mm")
        z_free = sem("z_free")
        gelu_done = sem("gelu_done")
        h_chain = sem("h_chain")
        var_done = sem("var_done")
        mean_ready = sem("mean_ready")
        centred = sem("centred")
        hn_ready = sem("hn_ready")
        scale2_ready = sem("scale2_ready")
        th_mm = sem("th_mm")
        th_hi = sem("th_hi")
        th_free = sem("th_free")
        o_mm = sem("o_mm")
        o_free = sem("o_free")
        stored = [sem(f"stored{i}") for i in range(4)]

        JOBS_AT = {0: [("V", 1, 0), ("Q", 2, 0)], 1: [("O", 4, -1), ("V", 2, 0)], 2: [("O", 5, -1), ("Q", 3, 0)],
                   3: [("O", 6, -1), ("V", 3, 0)], 4: [("O", 7, -1), ("K", 2, 0)], 5: [("K", 3, 0), ("Q", 4, 0)],
                   6: [("Q", 5, 0)], 7: [("Q", 6, 0)], 8: [("Q", 7, 0)], 9: [("X", 0, 1), ("X", 1, 1), ("O", 0, 0)],
                   10: [("O", 1, 0)], 11: [("O", 2, 0), ("K", 0, 1)], 12: [("O", 3, 0), ("K", 1, 1)], 13: [("Q", 0, 1)], 14: [("Q", 1, 1)], 15: [("V", 0, 1)]}
        LN_STEP, POW_STEP, XN_STEP, HALO_STEP = 5, 5, 7, 8
        ORDER = [j for s in range(UNITS) for j in JOBS_AT.get(s, [])]
        HI_ORDER = [j for j in ORDER if j[0] in "QXK"]
        JOBS, HIS = len(ORDER), len(HI_ORDER)
        NEXT_JOBS = sum(j[2] == 1 for j in ORDER)
        NEXT_HIS = sum(j[2] == 1 for j in HI_ORDER)
        assert JOBS % 2 == 0 and KO == 2 * NKV and NQ == NKV == 4
        PRE, FIRST, MID, LAST, DRAIN = range(5)
        ON = {-1: (MID, LAST, DRAIN), 0: (FIRST, MID, LAST), 1: (PRE, FIRST, MID)}

        def has(phase, rel):
            return phase in ON[rel]

        def at(b, per_batch, offset):
            return b[0] * per_batch + (b[1] * per_batch + offset)

        def jobs_of(phase, s):
            return [j for j in JOBS_AT.get(s, []) if has(phase, j[2])]

        def job_offset(phase, job):
            n = [j for j in ORDER if has(phase, j[2])].index(job)
            return n + (JOBS if phase == PRE else NEXT_JOBS if phase == FIRST else
                        NEXT_JOBS - 4 if phase in (MID, LAST) else -4)

        def hi_offset(phase, job):
            n = [j for j in HI_ORDER if has(phase, j[2])].index(job)
            return n + (HIS if phase == PRE else NEXT_HIS)

        def job_done(phase, b, kind, i):
            job = [j for j in ORDER if j[:2] == (kind, i)][0]
            if job[2] == 1:
                before = {FIRST: PRE, MID: MID, LAST: MID}[phase]
                return at(b, JOBS, job_offset(before, job) - JOBS + 3)
            return at(b, JOBS, job_offset(phase, job) + 3)

        PAIRS = 2 * UNITS
        HALOS = UNITS - NKV
        ALL_JOBS = B * JOBS

        def halos_before(u):
            return u - (u // NQ + 1)

        def batch_ring(eng, body):
            body(PRE, (0, -1))
            body(FIRST, (0, 0))
            with eng.Fori(0, B - 2) as r:
                body(MID, (r, 1))
            body(LAST, (0, B - 1))
            body(DRAIN, (0, B))

        def active(n, t):
            return not isinstance(n, int) or 0 <= t < NT

        def tile_loop(eng, step):
            for k in range(-2, 3):
                step(0, k)
            with eng.Fori(0, (NT - 8) // 4) as n:
                for k in range(3, 7):
                    step(n, k)
            for k in range(NT - 5, NT + 3):
                step(0, k)

        block = ctx.enter_context(nc.Block())

        @block.sync
        def _(sp):
            sp.dma_start(st_w1[:, :, :], w1.rearrange("(n p) d -> p n d", p=P)).then_inc(w_loaded[1], 16)
            sp.dma_start(st_w2[:, :, :], w2.rearrange("(n p) h -> p n h", p=P)).then_inc(w_loaded[2], 16)
            with nc.allow_non_contiguous_dma(reason="per-partition vectors of the layer norms"):
                sp.dma_start(lnb1[:, :], ln1_b.rearrange("(k p) -> p k", p=P)).then_inc(w_loaded[3], 16)
                sp.dma_start(lnb2[:, :], ln2_b.rearrange("(k p) -> p k", p=P)).then_inc(w_loaded[3], 16)
            with sp.Fori(0, B) as b:
                sp.wait_ge(x_loaded, b * 16 + 16)
                sp.dma_start(x_all[:, bass.ds(b * NQ, NQ), :], x_tiles[:, bass.ds(b * NQ, NQ), :])\
                  .then_inc(x_loaded, 16)
            def swap_keys(count, m):
                sp.wait_ge(job_free, count)
                for src, dst in ((k_hi, ks_hi), (k_lo, ks_lo)):
                    sp.dma_start(dst[0:HD, m, :].bitcast(F32), src[HD:P, m, :].bitcast(F32)).then_inc(k_swapped, 16)
                    sp.dma_start(dst[HD:P, m, :].bitcast(F32), src[0:HD, m, :].bitcast(F32)).then_inc(k_swapped, 16)

            def body(phase, b):
                for s in range(UNITS):
                    for job in jobs_of(phase, s):
                        if job[0] == "K" and job[1] % 2:
                            swap_keys(at(b, JOBS, job_offset(phase, job) + 3), job[1] // 2)

            batch_ring(sp, body)
            sp.wait_ge(job_free, 2 + ALL_JOBS)
            for dst, src in ((bias1, b1), (bias2, b2), (gain1, ln1_g), (gain2, ln2_g)):
                sp.dma_start(dst[:, :], src.partition_broadcast(P)).then_inc(ffn_loaded, 16)
            with sp.Fori(0, B) as c:
                for j in range(4):
                    sp.wait_ge(o_free, c * 4 + (1 + j + 1))
                    sp.dma_start(out_tiles[:, bass.ds(c * 4 + j, 1), :], f_out[:, j:j + 1, :])\
                      .then_inc(stored[j], 16)
            for j in range(4):
                sp.wait_ge(stored[j], 16 + 16 * B)

        @block.gpsimd
        def _(pool):
            def pool_gate():
                pool.tensor_tensor(gate[:, 0:1], ones[:, 0:1], ones[:, 0:1], ALU.mult)

            n = [0]

            def link(ins):
                n[0] += 1
                ins.then_inc(pool_consts, 1)
                pool.wait_ge(pool_consts, n[0])

            pool.memset(ones[:, :], 1.0)
            pool.memset(neg_half[:, :], -0.5)
            for m in (ident, ident_bf):
                link(pool.memset(m[:, :], 0.0))
                link(pool.affine_select(out=m[:, :], in_=m[:, :], compare_op=ALU.not_equal, fill=1.0,
                                        base=0, pattern=[[-1, P]], channel_multiplier=1))
            for m in (mask_first, mask_rest):
                link(pool.memset(m[:, :], 0.0))
                link(pool.affine_select(out=m[:, 0:P], in_=m[:, 0:P], compare_op=ALU.is_ge, fill=MASKED,
                                        base=0, pattern=[[-1, P]], channel_multiplier=1))
                lo = SINK if m is mask_first else 0
                link(pool.affine_select(out=m[:, lo:P], in_=m[:, lo:P], compare_op=ALU.is_ge, fill=MASKED,
                                        base=lo + WINDOW - 1, pattern=[[1, P - lo]], channel_multiplier=-1))
            link(pool.affine_select(out=mask_rest[:, P:P + WINDOW], in_=mask_rest[:, P:P + WINDOW],
                                    compare_op=ALU.is_ge, fill=MASKED, base=-1, pattern=[[1, WINDOW]],
                                    channel_multiplier=-1))
            pool.memset(gate[:, 31:32], 0.0).then_inc(masks_ready, 1)
            pool.wait_ge(setup_done, 1)
            for xt in (xt_hi, xt_lo):
                for k in range(KD):
                    pool.memset(xt[:, k, 0, P:KEYS].bitcast(F32), 0.0)

            def power(b):
                pool.wait_ge(var_ready, at(b, 1, 2))
                pool.tensor_tensor(rstd[:, :], var_eps[:, :], neg_half[:, 0:NQ], ALU.pow).then_inc(rstd_ready, 1)

            def halo_columns(count):
                pool.wait_ge(job_free, count)
                pool_gate()
                for k in range(KD):
                    for xt in (xt_hi, xt_lo):
                        pool.tensor_copy(xt[:, k, 1:NQ, P:P + WINDOW], xt[:, k, 0:NQ - 1, WINDOW:P])
                        last = pool.tensor_copy(xt[:, k, 1:NQ, P + WINDOW:KEYS],
                                                xt[:, k, 0:1, 0:SINK].to_broadcast([P, NQ - 1, SINK]))
                last.then_inc(ext_ready, 1)

            def body(phase, b):
                for s in range(UNITS):
                    if has(phase, 0):
                        w = KEYS if s % NQ else P
                        pool.wait_ge(rec_ready, at(b, UNITS, 2 + s + 1))
                        pool.tensor_tensor(probs[:, s % 4, :, 0:w], probs[:, s % 4, :, 0:w],
                                           row_rec[:, s % 2, :].unsqueeze(2).to_broadcast([P, REP, w]), ALU.mult)\
                            .then_inc(probs_ready, 1)
                    if has(phase, 1) and s == POW_STEP:
                        power(b)
                    if has(phase, 1) and s == HALO_STEP:
                        halo_columns(at(b, JOBS, job_offset(phase, ("X", KD - 1, 1)) + 3))

            batch_ring(pool, body)

            pool.wait_ge(f_pow_in, 1)
            pool.tensor_tensor(f_r1[:, :], f_var[:, :], neg_half[:, :], ALU.pow).then_inc(f_pow_out, 1)
            pool.wait_ge(f_pow_in, 2)
            pool.tensor_tensor(f_r2[:, :], f_var2[:, :], neg_half[:, :], ALU.pow).then_inc(f_pow_out, 1)
            pool.wait_ge(f_chain, 6)

            def step(n, k):
                t = k - 1
                if active(n, t):
                    pool.wait_ge(var_done, n * 4 + (t + 1))
                    pool.tensor_tensor(scale2[:, t % 4:t % 4 + 1], h_var[:, t % 4:t % 4 + 1], neg_half[:, 0:1],
                                       ALU.pow).then_inc(scale2_ready, 1)
                    pool.wait_ge(centred, n * 4 + (t + 1))
                    pool.tensor_tensor(hid[:, t % 4, :], hid[:, t % 4, :], gain2[:, :], ALU.mult).then_inc(hn_ready, 1)
                    pool.tensor_tensor(f_xb[:, t % 4:t % 4 + 1, :], x_all[:, bass.ds(n * 4 + t, 1), :],
                                       bias2[:, :].unsqueeze(1), ALU.add).then_inc(xb_ready, 1)

            tile_loop(pool, step)

        @block.scalar
        def _(act):
            for dst, src in ((st_wq, Wq), (st_wk, Wk), (st_wv, Wv), (st_wo, Wo)):
                act.dma_start(dst[:, :, :], src.rearrange("(k p) n -> p k n", p=P)).then_inc(w_loaded[0], 16)
            act.wait_ge(w_loaded[1], 16)
            act.activation(abs_w[:, 0, :], st_w1[:, :, :].rearrange("p n d -> p (n d)"), ACT.Abs).then_inc(abs_ready, 1)
            act.wait_ge(w_loaded[2], 16)
            act.activation(abs_w[:, 1, :], st_w2[:, :, :].rearrange("p n d -> p (n d)"), ACT.Abs).then_inc(abs_ready, 1)
            act.wait_ge(w_loaded[0], 64)
            for hi, src in ((wq_hi, st_wq), (wk_hi, st_wk), (wv_hi, st_wv), (wo_hi, st_wo)):
                act.activation(hi[:, :, :], src[:, :, :], ACT.Copy).then_inc(hi_ready, 1)
            act.wait_ge(setup_done, 1)

            def hi_part(phase, b, job):
                kind, i, _ = job
                offset = job_offset(phase, job)
                ps = ps_job[offset % 2]
                act.wait_ge(job_mm, at(b, JOBS, offset + 1))
                if kind == "X":
                    act.activation(xt_hi[:, i, :, 0:P], ps[:, :].rearrange("p (n t) -> p n t", n=NQ), ACT.Copy)\
                       .then_inc(job_hi, 1)
                elif kind == "K":
                    m, h = divmod(i, 2)
                    act.activation(k_hi[:, m, h * HALF:(h + 1) * HALF], ps[:, 0:HALF], ACT.Copy).then_inc(job_hi, 1)
                elif kind == "Q":
                    act.activation(q_hi[:, i // 2 % 2, i % 2, :], ps[:, :], ACT.Copy, scale=SCALE).then_inc(job_hi, 1)

            def exps(b, u):
                w = KEYS if u % NQ else P
                act.wait_ge(score_free, at(b, PAIRS, 2 + 2 * u + 2))
                act.wait_ge(rec_ready, at(b, UNITS, u + 1))
                act.wait_ge(pt_mm, at(b, UNITS, u + 1))
                for j in range(REP):
                    last = act.activation(probs[:, u % 4, j, 0:w], scores[:, u % 2, j, 0:w], ACT.Exp,
                                          bias=neg_max[:, u % 2, j:j + 1], scale=-1.0,
                                          accum_out=row_sum[:, u % 2, j:j + 1])
                last.then_inc(exp_done, 1)

            def copy_pt(b, u):
                act.wait_ge(pt_mm, at(b, UNITS, 4 + u + 1))
                act.wait_ge(y_mm, at(b, UNITS, u + 1))
                act.activation(pt_own[:, u % 2, :], ps_pt_own[:, :], ACT.Copy).then_inc(pt_own_done, 1)

            def y_hi_part(phase, b, u):
                g, qb = divmod(u % UNITS, NQ)
                act.wait_ge(y_mm, at(b, UNITS, 2 + u + 1))
                if 0 <= u < NQ and has(phase, -1):
                    act.wait_ge(job_mm, at(b, JOBS, job_offset(phase, ("O", NQ + qb, -1)) + 1))
                elif u >= 0 and g == 2:
                    act.wait_ge(job_mm, at(b, JOBS, job_offset(phase, ("O", qb, 0)) + 1))
                for half in range(2):
                    rows = slice(half * HD, (half + 1) * HD)
                    src = ps_y[u % 2][rows, :].rearrange("p (m h q) -> p m h q", m=2, h=2)[:, :, half, :]
                    last = act.activation(y_hi[rows, qb, g % 2 * 2:g % 2 * 2 + 2, :], src, ACT.Copy)
                last.then_inc(y_hi_done, 1)

            def body(phase, b):
                for s in range(UNITS):
                    if has(phase, 0):
                        exps(b, s)
                    if has(phase, 0 if s >= 2 else -1):
                        copy_pt(b, s - 2)
                    if has(phase, 0 if s >= 3 else -1):
                        y_hi_part(phase, b, s - 3)
                    for job in jobs_of(phase, s):
                        if job in HI_ORDER:
                            hi_part(phase, b, job)

            batch_ring(act, body)

            act.wait_ge(job_free, 2 + ALL_JOBS)

            def step(n, k):
                t = k - 3
                if active(n, t):
                    for h in range(2):
                        act.wait_ge(th_mm, n * 8 + (2 * t + h + 1))
                        act.activation(ht_hi[:, 512 * h:512 * h + 512], ps_th[h][:, :], ACT.Copy).then_inc(th_hi, 1)
                t = k + 1
                if active(n, t):
                    act.wait_ge(tx_mm, n * 4 + (t + 1))
                    act.activation(fx_hi[:, t % 2, :], ps_tx[:, 0:D], ACT.Copy).then_inc(tx_hi, 1)
                t = k
                if active(n, t):
                    act.wait_ge(z_free, n * 4 + (2 + t + 1))
                    act.activation(hid[:, t % 4, :], hid[:, t % 4, :], ACT.Gelu).then_inc(gelu_done, 1)
                t = k - 1
                if active(n, t):
                    act.wait_ge(mean_ready, n * 4 + (t + 1))
                    act.activation(hid[:, t % 4, :], hid[:, t % 4, :], ACT.Identity,
                                   bias=h_negmean[:, t % 4:t % 4 + 1]).then_inc(centred, 1)

            tile_loop(act, step)

        @block.vector
        def _(dve):
            def dve_gate(i=0):
                dve.memset(gate[:, 1 + i:2 + i], 0.0)

            for i, (s, n) in enumerate(((job_free, 2), (score_free, 2), (exp_done, 2), (rec_ready, 2), (probs_ready, 2),
                         (pt_mm, 4), (pt_own_done, 1), (pt_halo_done, 1), (y_mm, 2), (y_free, 2),
                         (tx_free, 1), (th_free, 2), (z_free, 2), (o_free, 1), (x_loaded, 16),
                         *((x, 16) for x in stored))):
                dve.memset(gate[:, 8 + i:9 + i], 0.0).then_inc(s, n)
            steps = [0]

            def link(ins):
                steps[0] += 1
                ins.then_inc(dve_step, 1)
                dve.wait_ge(dve_step, steps[0])

            dve.wait_ge(masks_ready, 1)
            dve.wait_ge(abs_ready, 2)
            link(dve.tensor_reduce(abs_64[:, :, :], abs_w[:, :, :].rearrange("p w (a c) -> p w a c", a=64), AX_X, ALU.add))
            link(dve.tensor_reduce(abs_8[:, :, :], abs_64[:, :, :].rearrange("p w (a c) -> p w a c", a=8), AX_X, ALU.add))
            dve.tensor_reduce(wsum[:, :], abs_8[:, :, :], AX_X, ALU.add).then_inc(sums_ready, 1)
            dve.wait_ge(total_ready, 1)
            link(dve.tensor_reduce(tot_row[:, :], ps_job[0][0:2, 0:P].rearrange("w (a c) -> w a c", a=8), AX_X, ALU.add))
            link(dve.tensor_reduce(tot[:, :], tot_row[:, :], AX_X, ALU.add))
            dve.tensor_scalar(tot_diag[:, :], ident[0:2, 0:2], tot[:, 0:1], None, ALU.mult).then_inc(sums_ready, 1)
            dve.wait_ge(total_ready, 2)
            link(dve.tensor_scalar(wmean[:, :], ps_job[0][:, 0:2], 1.0 / (HID * D), 1e-5, ALU.mult, ALU.max))
            link(dve.reciprocal(wscale[:, :], wmean[:, :]))
            link(dve.reciprocal(winv[:, :], wscale[:, :]))
            link(dve.tensor_tensor(wscale_sq[:, :], wscale[:, :], wscale[:, :], ALU.mult))
            for i, st in enumerate((st_w1, st_w2)):
                flat = st[:, :, :].rearrange("p n d -> p (n d)")
                link(dve.tensor_scalar(pos[:, :], flat, wscale[:, i:i + 1], 0.5, ALU.mult, ALU.is_gt))
                link(dve.tensor_scalar(neg[:, :], flat, wscale[:, i:i + 1], -0.5, ALU.mult, ALU.is_lt))
                dve.tensor_tensor(tern[:, i, :], pos[:, :], neg[:, :], ALU.subtract).then_inc(tern_ready, 1)
                dve.wait_ge(tern_ready, i + 1)
            for i, (lo, hi, src) in enumerate(((wq_lo, wq_hi, st_wq), (wk_lo, wk_hi, st_wk),
                                               (wv_lo, wv_hi, st_wv), (wo_lo, wo_hi, st_wo))):
                dve.wait_ge(hi_ready, i + 1)
                dve.tensor_tensor(lo[:, :, :], src[:, :, :], hi[:, :, :].bitcast(F32), ALU.subtract)
            for i, dst in enumerate((t1T[:, 0, :], t1T[:, 1, :],
                                     t2T[:, 0:KF // 2, :].rearrange("p k d -> p (k d)"),
                                     t2T[:, KF // 2:KF, :].rearrange("p k d -> p (k d)"))):
                dve.wait_ge(tern_T, i + 1)
                dve.tensor_copy(dst, (ps_score + ps_y)[i][:, :].bitcast(BF16)).then_inc(tT_ready, 1)
            dve.memset(gate[:, 7:8], 0.0).then_inc(setup_done, 1)
            dve.wait_ge(setup_done, 1)

            def lo_part(phase, b, job):
                kind, i, _ = job
                offset = job_offset(phase, job)
                ps = ps_job[offset % 2]
                if job in HI_ORDER:
                    dve.wait_ge(job_hi, at(b, HIS, hi_offset(phase, job) + 1))
                else:
                    dve.wait_ge(job_mm, at(b, JOBS, offset + 1))
                if kind == "X":
                    ins = dve.tensor_tensor(xt_lo[:, i, :, 0:P], ps[:, :].rearrange("p (n t) -> p n t", n=NQ),
                                            xt_hi[:, i, :, 0:P].bitcast(F32), ALU.subtract)
                elif kind == "K":
                    m, h = divmod(i, 2)
                    cols = slice(h * HALF, (h + 1) * HALF)
                    ins = dve.tensor_tensor(k_lo[:, m, cols], ps[:, 0:HALF], k_hi[:, m, cols].bitcast(F32),
                                            ALU.subtract)
                elif kind == "Q":
                    ins = dve.scalar_tensor_tensor(out=q_lo[:, i // 2 % 2, i % 2, :], in0=ps[:, :], scalar=SCALE,
                                                   in1=q_hi[:, i // 2 % 2, i % 2, :].bitcast(F32), op0=ALU.mult, op1=ALU.subtract)
                elif kind == "V":
                    own = ps[:, 0:NKV * HD].rearrange("p (g o d) -> p g o d", g=NKV, o=1)
                    ins = dve.tensor_copy(v_own[:, i, :, :, :], own.to_broadcast([P, NKV, 2, HD]))
                    if i:
                        halo = ps[0:HALO, 256:256 + NKV * HD].rearrange("p (g o d) -> p g o d", g=NKV, o=1)
                        ins = dve.tensor_copy(v_halo[:, i - 1, :, :, :], halo.to_broadcast([HALO, NKV, 2, HD]))
                else:
                    row = x_all[:, bass.ds(at(b, NQ, i if i < NQ else i - 2 * NQ), 1), :].rearrange("p o d -> p (o d)")
                    ins = dve.tensor_tensor(row, row, ps[:, 0:D], ALU.add)
                ins.then_inc(job_free, 1)

            def result_stats(phase, b, qb):
                dve.wait_ge(job_free, at(b, JOBS, job_offset(phase, ("O", NQ + qb, -1)) + 3))
                row = x_all[:, bass.ds(at(b, NQ, qb - NQ), 1), :].rearrange("p o d -> p (o d)")
                dve.bn_stats(x_stats[:, bass.ds(at(b, NQ, qb - NQ), 1), :].rearrange("p o s -> p (o s)"), row)

            def mask_and_max(b, u, pair):
                w = KEYS if u % NQ else P
                mask = mask_rest if u % NQ else mask_first
                if pair == 0:
                    dve.wait_ge(exp_done, at(b, UNITS, u + 1))
                dve.wait_ge(score_mm, at(b, PAIRS, 2 * u + pair + 1))
                dve_gate(1 + (2 * u + pair) % 4)
                for j in (pair, pair + 2):
                    last = dve.tensor_tensor_reduce(
                        scores[:, u % 2, j, 0:w], ps_score[pair][:, (j // 2) * 256:(j // 2) * 256 + w],
                        mask[:, 0:w], -1.0, BIG, ALU.add, ALU.min, neg_max[:, u % 2, j:j + 1])
                last.then_inc(score_free, 1)

            def reciprocals(b, u):
                dve.wait_ge(exp_done, at(b, UNITS, 2 + u + 1))
                dve.wait_ge(probs_ready, at(b, UNITS, u + 1))
                dve.tensor_scalar(row_rec[:, u % 2, :], row_sum[:, u % 2, :], TINY, None, ALU.max)\
                    .then_inc(rec_chain, 1)
                dve.wait_ge(rec_chain, at(b, UNITS, u + 1))
                dve.reciprocal(row_rec[:, u % 2, :], row_rec[:, u % 2, :]).then_inc(rec_ready, 1)

            def copy_pt(b, u):
                dve.wait_ge(pt_mm, at(b, UNITS, 4 + u + 1))
                dve.wait_ge(y_mm, at(b, UNITS, u + 1))
                dve.tensor_copy(pt_halo[:, u % 2, :], ps_pt_halo[0:HALO, :]).then_inc(pt_halo_done, 1)

            def y_lo_part(b, u):
                g, qb = divmod(u % UNITS, NQ)
                dve.wait_ge(y_hi_done, at(b, UNITS, u + 1))
                for half in range(2):
                    rows = slice(half * HD, (half + 1) * HD)
                    src = ps_y[u % 2][rows, :].rearrange("p (m h q) -> p m h q", m=2, h=2)[:, :, half, :]
                    last = dve.tensor_tensor(y_lo[rows, qb, g % 2 * 2:g % 2 * 2 + 2, :], src,
                                             y_hi[rows, qb, g % 2 * 2:g % 2 * 2 + 2, :].bitcast(F32), ALU.subtract)
                last.then_inc(y_free, 1)

            CHAIN = 2

            def token_stats(b):
                dve.wait_ge(x_loaded, at(b, 16, 48))
                for n in range(NQ):
                    row = x_all[:, bass.ds(at(b, NQ, NQ + n), 1), :].rearrange("p o d -> p (o d)")
                    last = dve.bn_stats(stats[:, n, :], row)
                last.then_inc(dve_chain, 1)
                dve.wait_ge(dve_chain, at(b, CHAIN, CHAIN + 1))
                dve_gate()
                for n in range(NQ):
                    last = dve.bn_aggr(moments[:, n, :], stats[:, n, :])
                last.then_inc(dve_chain, 1)
                dve.wait_ge(dve_chain, at(b, CHAIN, CHAIN + 2))
                dve.tensor_scalar(var_eps[:, :], moments[:, :, 1], LN_EPS, None, ALU.add).then_inc(var_ready, 1)

            def normalise(b):
                dve.wait_ge(rstd_ready, at(b, 1, 2))
                for n in range(NQ):
                    row = x_all[:, bass.ds(at(b, NQ, NQ + n), 1), :].rearrange("p o d -> p (o d)")
                    last = dve.tensor_scalar(xn[:, n, :], row, moments[:, n, 0:1], rstd[:, n:n + 1],
                                             ALU.subtract, ALU.mult)
                last.then_inc(xn_ready, 1)

            def body(phase, b):
                for s in range(UNITS):
                    if has(phase, 0 if s >= 1 else -1):
                        reciprocals(b, s - 1)
                    if has(phase, 0):
                        mask_and_max(b, s, 0)
                        mask_and_max(b, s, 1)
                    if (s - 2) % NQ and has(phase, 0 if s >= 2 else -1):
                        copy_pt(b, s - 2)
                    if has(phase, 0 if s >= 4 else -1):
                        y_lo_part(b, s - 4)
                    for kind, i, _ in jobs_of(phase, s - 1):
                        if kind == "O" and i >= NQ:
                            result_stats(phase, b, i - NQ)
                    for job in jobs_of(phase, s):
                        lo_part(phase, b, job)
                    if has(phase, 1) and s == LN_STEP:
                        token_stats(b)
                    if has(phase, 1) and s == XN_STEP:
                        normalise(b)

            batch_ring(dve, body)

            dve.wait_ge(job_free, 2 + ALL_JOBS)
            links = [0]

            def step_link(ins):
                links[0] += 1
                ins.then_inc(f_chain, 1)
                dve.wait_ge(f_chain, links[0])

            step_link(dve.memset(gate[:, 6:7], 0.0))
            for t in range(NT):
                last = dve.bn_aggr(f_moments[:, t, :], x_stats[:, t, :])
            step_link(last)
            dve.tensor_scalar(f_var[:, :], f_moments[:, :, 1], LN_EPS, None, ALU.add).then_inc(f_pow_in, 1)
            dve.wait_ge(f_pow_out, 1)
            step_link(dve.tensor_tensor(f_var2[:, :], f_moments[:, :, 1], f_r1[:, :], ALU.mult))
            step_link(dve.tensor_tensor(f_var2[:, :], f_var2[:, :], f_r1[:, :], ALU.mult))
            dve.tensor_scalar(f_var2[:, :], f_var2[:, :], LN_EPS, None, ALU.add).then_inc(f_pow_in, 1)
            dve.wait_ge(f_pow_out, 2)
            step_link(dve.tensor_tensor(scale1[:, :], f_r1[:, :], f_r2[:, :], ALU.mult))
            dve.tensor_scalar(scale1[:, :], scale1[:, :], winv[:, 0:1], None, ALU.mult)
            dve.wait_ge(ffn_loaded, 64)
            dve.wait_ge(fbias_mm, 1)
            dve.scalar_tensor_tensor(out=bias1[:, :], in0=ps_z[0][:, :], scalar=winv[:, 0:1], in1=bias1[:, :],
                                     op0=ALU.mult, op1=ALU.add)
            step_link(dve.scalar_tensor_tensor(out=bias2[:, :], in0=ps_o[:, 0:D], scalar=winv[:, 1:2],
                                               in1=bias2[:, :], op0=ALU.mult, op1=ALU.add))
            assert links[0] == 6

            def step(n, k):
                t = k - 3
                if active(n, t):
                    for h in range(2):
                        dve.wait_ge(th_hi, n * 8 + (2 * t + h + 1))
                        dve.tensor_tensor(ht_lo[:, 512 * h:512 * h + 512], ps_th[h][:, :],
                                          ht_hi[:, 512 * h:512 * h + 512].bitcast(F32), ALU.subtract)\
                            .then_inc(th_free, 1)
                t = k + 1
                if active(n, t):
                    dve.wait_ge(tx_hi, n * 4 + (t + 1))
                    dve.tensor_tensor(fx_lo[:, t % 2, :], ps_tx[:, 0:D], fx_hi[:, t % 2, :].bitcast(F32),
                                      ALU.subtract).then_inc(tx_free, 1)
                t = k - 1
                if active(n, t):
                    dve.wait_ge(gelu_done, n * 4 + (t + 1))
                    dve.bn_stats(h_stats[:, t % 4, 0, :], hid[:, t % 4, 0:512])
                    dve.bn_stats(h_stats[:, t % 4, 1, :], hid[:, t % 4, 512:1024]).then_inc(h_chain, 1)
                t = k
                if active(n, t):
                    dve.wait_ge(z_mm, n * 4 + (t + 1))
                    dve.scalar_tensor_tensor(out=hid[:, t % 4, :], in0=ps_z[t % 2][:, :],
                                             scalar=scale1[:, bass.ds(n * 4 + t, 1)], in1=bias1[:, :],
                                             op0=ALU.mult, op1=ALU.add).then_inc(z_free, 1)
                t = k - 1
                if active(n, t):
                    dve.wait_ge(h_chain, n * 8 + (2 * t + 1))
                    dve_gate()
                    dve.bn_aggr(h_moments[:, t % 4, :], h_stats[:, t % 4, :, :].rearrange("p a s -> p (a s)"))\
                        .then_inc(h_chain, 1)
                    dve.wait_ge(h_chain, n * 8 + (2 * t + 2))
                    dve.tensor_scalar(h_negmean[:, t % 4:t % 4 + 1], h_moments[:, t % 4, 0:1], -1.0, None,
                                      ALU.mult).then_inc(mean_ready, 1)
                    dve.tensor_scalar(h_var[:, t % 4:t % 4 + 1], h_moments[:, t % 4, 1:2], LN_EPS,
                                      wscale_sq[:, 1:2], ALU.add, ALU.mult).then_inc(var_done, 1)
                t = k - 3
                if active(n, t):
                    dve.wait_ge(o_mm, n * 4 + (t + 1))
                    dve.wait_ge(scale2_ready, n * 4 + (t + 1))
                    dve.wait_ge(xb_ready, n * 4 + (t + 1))
                    dve.wait_ge(stored[t % 4], n * 16 + (16 + 16 * (t // 4)))
                    dve.scalar_tensor_tensor(out=f_out[:, t % 4, :], in0=ps_o[:, 0:D],
                                             scalar=scale2[:, t % 4:t % 4 + 1], in1=f_xb[:, t % 4, :],
                                             op0=ALU.mult, op1=ALU.add).then_inc(o_free, 1)
                t = k + 2
                if active(n, t):
                    row = x_all[:, bass.ds(n * 4 + t, 1), :].rearrange("p o d -> p (o d)")
                    dve.scalar_tensor_tensor(out=f_xm[:, t % 2, :], in0=row,
                                             scalar=f_moments[:, bass.ds(n * 4 + t, 1), 0:1].rearrange("p o d -> p (o d)"),
                                             in1=gain1[:, :], op0=ALU.subtract, op1=ALU.mult).then_inc(xm_ready, 1)

            tile_loop(dve, step)

        @block.tensor
        def _(pe):
            pe.wait_ge(masks_ready, 1)
            pe.wait_ge(sums_ready, 1)
            pe.transpose(ps_job[0][0:2, 0:P], wsum[:, :], ident[:, :]).then_inc(total_ready, 1)
            pe.wait_ge(sums_ready, 2)
            pe.matmul(ps_job[0][:, 0:2], ones[0:2, :], tot_diag[:, :], start=True, stop=True).then_inc(total_ready, 1)
            for i in range(4):
                bank = (ps_score + ps_y)[i][:, :].bitcast(BF16)
                pe.wait_ge(tern_ready, i // 2 + 1)
                for n in range(KF):
                    if i < 2:
                        src = tern[:, 0, n * D + i * P:n * D + (i + 1) * P]
                    else:
                        k, d = (i - 2) * (KF // 2) + n // 2, n % 2
                        src = tern[:, 1, d * HID + k * P:d * HID + (k + 1) * P]
                    last = pe.transpose(bank[:, n * P:(n + 1) * P], src, ident_bf[:, :])
                last.then_inc(tern_T, 1)
            pe.wait_ge(setup_done, 1)

            def split_matmul(dst, terms):
                n = len(terms)
                for i, (s_hi, s_lo, m_hi, m_lo) in enumerate(terms):
                    pe.matmul(dst, s_hi, m_hi, start=(i == 0), stop=False)
                    pe.matmul(dst, s_hi, m_lo, start=False, stop=False)
                    last = pe.matmul(dst, s_lo, m_hi, start=False, stop=(i == n - 1))
                return last

            def scores_of(phase, b, u, pair):
                g, qb = divmod(u, NQ)
                w = KEYS if qb else P
                pe.wait_ge(score_free, at(b, PAIRS, 2 * u + pair + 1))
                if pair == 0 and qb == 0:
                    pe.wait_ge(job_free, job_done(phase, b, "Q", 2 * g + 1))
                    if g % 2 == 0:
                        pe.wait_ge(k_swapped, at(b, 64 * KM, 64 * (g // 2 + 1)))
                half = pair
                for j in (pair, pair + 2):
                    rows = slice(half * HD, (half + 1) * HD)
                    kh, kl = (k_hi, k_lo) if g % 2 == half else (ks_hi, ks_lo)
                    last = split_matmul(ps_score[pair][:, (j // 2) * 256:(j // 2) * 256 + w],
                                        [(q_hi[rows, g % 2, j // 2, qb * P:(qb + 1) * P],
                                          q_lo[rows, g % 2, j // 2, qb * P:(qb + 1) * P],
                                          kh[rows, g // 2, qb * KEYS:qb * KEYS + w],
                                          kl[rows, g // 2, qb * KEYS:qb * KEYS + w])])
                last.then_inc(score_mm, 1)

            def transpose_probs(b, u):
                pe.wait_ge(probs_ready, at(b, UNITS, 2 + u + 1))
                pe.wait_ge(pt_own_done, at(b, UNITS, u + 1))
                if u % NQ:
                    pe.wait_ge(pt_halo_done, at(b, HALOS, halos_before(u) + 1))
                for j in range(REP):
                    last = pe.transpose(ps_pt_own[:, j * P:(j + 1) * P], probs[:, u % 4, j, 0:P], ident[:, :])
                if u % NQ:
                    for j in range(REP):
                        last = pe.transpose(ps_pt_halo[0:HALO, j * P:(j + 1) * P], probs[:, u % 4, j, P:KEYS],
                                            ident[:, :])
                last.then_inc(pt_mm, 1)

            def outputs_of(phase, b, u):
                g, qb = divmod(u % UNITS, NQ)
                pe.wait_ge(pt_own_done, at(b, UNITS, 1 + u + 1))
                if qb:
                    pe.wait_ge(pt_halo_done, at(b, HALOS, 1 + halos_before(u) + 1))
                pe.wait_ge(y_free, at(b, UNITS, u + 1))
                if 0 <= u < NQ:
                    pe.wait_ge(job_free, job_done(phase, b, "V", qb))
                v = v_own[:, qb, g, :, :].rearrange("p t d -> p (t d)")
                last = pe.matmul(ps_y[u % 2][:, :], v, pt_own[:, u % 2, :], start=True, stop=(qb == 0))
                if qb:
                    v = v_halo[:, qb - 1, g, :, :].rearrange("p t d -> p (t d)")
                    last = pe.matmul(ps_y[u % 2][:, :], v, pt_halo[:, u % 2, :], start=False, stop=True)
                last.then_inc(y_mm, 1)

            def job_product(phase, b, job):
                kind, i, _ = job
                offset = job_offset(phase, job)
                ps = ps_job[offset % 2]
                pe.wait_ge(job_free, at(b, JOBS, offset + 1))
                if kind == "X":
                    pe.wait_ge(xn_ready, at(b, 1, 2))
                    for n in range(NQ):
                        last = pe.transpose(ps[:, n * P:(n + 1) * P], xn[:, n, i * P:(i + 1) * P], ident[:, :])
                elif kind == "K":
                    if i == 0:
                        pe.wait_ge(ext_ready, at(b, 1, 2))
                    m, h = divmod(i, 2)
                    cols = slice(h * (NQ // 2), (h + 1) * (NQ // 2))
                    last = split_matmul(ps[:, 0:HALF],
                                        [(wk_hi[:, k, m * P:(m + 1) * P], wk_lo[:, k, m * P:(m + 1) * P],
                                          xt_hi[:, k, cols, :], xt_lo[:, k, cols, :]) for k in range(KD)])
                elif kind == "V":
                    last = split_matmul(ps[:, 0:256],
                                        [(xt_hi[:, k, i, 0:P], xt_lo[:, k, i, 0:P], wv_hi[:, k, :], wv_lo[:, k, :])
                                         for k in range(KD)])
                    if i:
                        last = split_matmul(ps[0:HALO, 256:512],
                                            [(xt_hi[:, k, i, P:KEYS], xt_lo[:, k, i, P:KEYS],
                                              wv_hi[:, k, :], wv_lo[:, k, :]) for k in range(KD)])
                elif kind == "Q":
                    last = split_matmul(ps[:, :],
                                        [(wq_hi[:, k, i * P:(i + 1) * P], wq_lo[:, k, i * P:(i + 1) * P],
                                          xt_hi[:, k, :, 0:P], xt_lo[:, k, :, 0:P]) for k in range(KD)])
                else:
                    half, qb = divmod(i, NQ)
                    pe.wait_ge(y_free, at(b, UNITS, 2 + (qb - NQ if half else qb + NQ) + 1))
                    last = split_matmul(ps[:, 0:D], [(y_hi[:, qb, k, :], y_lo[:, qb, k, :], wo_hi[:, half * KO // 2 + k, :],
                                                      wo_lo[:, half * KO // 2 + k, :]) for k in range(KO // 2)])
                last.then_inc(job_mm, 1)

            def body(phase, b):
                for s in range(UNITS):
                    if has(phase, 0):
                        scores_of(phase, b, s, 0)
                        scores_of(phase, b, s, 1)
                    if has(phase, 0 if s >= 2 else -1):
                        transpose_probs(b, s - 2)
                    if has(phase, 0 if s >= 3 else -1):
                        outputs_of(phase, b, s - 3)
                    for job in jobs_of(phase, s):
                        job_product(phase, b, job)

            batch_ring(pe, body)

            pe.wait_ge(w_loaded[3], 32)
            pe.wait_ge(job_free, 2 + ALL_JOBS)
            for h in range(2):
                for k in range(KD):
                    pe.matmul(ps_z[0][:, 512 * h:512 * h + 512], lnb1[:, k:k + 1].to_broadcast([P, P]),
                              t1T[:, k, 512 * h:512 * h + 512].bitcast(F32), start=(k == 0), stop=(k == KD - 1))
            for k in range(KF):
                last = pe.matmul(ps_o[:, 0:D], lnb2[:, k:k + 1].to_broadcast([P, P]),
                                 t2T[:, k, :].bitcast(F32), start=(k == 0), stop=(k == KF - 1))
            last.then_inc(fbias_mm, 1)
            pe.wait_ge(f_chain, 6)

            def ternary_matmul(dst, terms):
                n = len(terms)
                for i, (a_hi, a_lo, w) in enumerate(terms):
                    pe.matmul(dst, a_hi, w, start=(i == 0), stop=False)
                    last = pe.matmul(dst, a_lo, w, start=False, stop=(i == n - 1))
                return last

            def step(n, k):
                t = k - 3
                if active(n, t):
                    pe.wait_ge(hn_ready, n * 4 + (t + 1))
                    for h in range(2):
                        pe.wait_ge(th_free, n * 8 + (2 * t + h + 1))
                        for i in range(4):
                            c = 4 * h + i
                            last = pe.transpose(ps_th[h][:, i * P:(i + 1) * P], hid[:, t % 4, c * P:(c + 1) * P],
                                                ident[:, :])
                        last.then_inc(th_mm, 1)
                t = k + 1
                if active(n, t):
                    pe.wait_ge(xm_ready, n * 4 + (t + 1))
                    pe.wait_ge(tx_free, n * 4 + (t + 1))
                    for i in range(KD):
                        last = pe.transpose(ps_tx[:, i * P:(i + 1) * P], f_xm[:, t % 2, i * P:(i + 1) * P],
                                            ident[:, :])
                    last.then_inc(tx_mm, 1)
                t = k
                if active(n, t):
                    pe.wait_ge(tx_free, n * 4 + (1 + t + 1))
                    pe.wait_ge(z_free, n * 4 + (t + 1))
                    for h in range(2):
                        last = ternary_matmul(ps_z[t % 2][:, 512 * h:512 * h + 512],
                                              [(fx_hi[:, t % 2, i * P:(i + 1) * P], fx_lo[:, t % 2, i * P:(i + 1) * P],
                                                t1T[:, i, 512 * h:512 * h + 512]) for i in range(KD)])
                    last.then_inc(z_mm, 1)
                t = k - 3
                if active(n, t):
                    pe.wait_ge(th_free, n * 8 + (2 + 2 * t + 2))
                    pe.wait_ge(o_free, n * 4 + (t + 1))
                    ternary_matmul(ps_o[:, 0:D], [(ht_hi[:, i * P:(i + 1) * P], ht_lo[:, i * P:(i + 1) * P],
                                                   t2T[:, i, :]) for i in range(KF)]).then_inc(o_mm, 1)

            tile_loop(pe, step)


_INS = ['L0_attn_X', 'L0_attn_Wq', 'L0_attn_Wk', 'L0_attn_Wv', 'L0_attn_Wo', 'L0_ffn_ln1_g', 'L0_ffn_ln1_b',
        'L0_ffn_w1', 'L0_ffn_b1', 'L0_ffn_ln2_g', 'L0_ffn_ln2_b', 'L0_ffn_w2', 'L0_ffn_b2']
_OUTS = [((8, 512, 256), 'float32')]


def kernel(**inputs):
    import numpy as _np
    import concourse.bacc as _bacc
    from concourse import mybir as _mybir
    from concourse.bass_utils import run_bass_kernel_spmd as _run

    nc = _bacc.Bacc("TRN2", target_bir_lowering=False, num_devices=1)
    arrays, args = {}, []
    for name in _INS:
        a = _np.ascontiguousarray(inputs[name])
        arrays[f"in_{name}_dram"] = a
        args.append(nc.dram_tensor(f"in_{name}_dram", a.shape, _mybir.dt.from_np(a.dtype), kind="ExternalInput").ap())
    for i, (shape, dtype) in enumerate(_OUTS):
        dt = _mybir.dt.from_np(_np.dtype(dtype))
        args.append(nc.dram_tensor(f"out_{i}_dram", shape, dt, kind="ExternalOutput").ap())
    layer_kernel(nc, *args)
    r = _run(nc, [arrays], core_ids=[0])
    return r.results[0]["out_0_dram"]
```

```python
from contextlib import ExitStack

import concourse.bass as bass
from concourse import mybir

P = 128
F32 = mybir.dt.float32
F32R = mybir.dt.float32r
BF16 = mybir.dt.bfloat16
ALU = mybir.AluOpType
ACT = mybir.ActivationFunctionType
AX_X = mybir.AxisListType.X

WINDOW = 64
SINK = 4
HD = 64
LN_EPS = 1e-5
MASKED = -1.0e30
TINY = 1.1754943508222875e-38
BIG = 3.0e38


def layer_kernel(nc, X, Wq, Wk, Wv, Wo, ln1_g, ln1_b, w1, b1, ln2_g, ln2_b, w2, b2, out):
    B, T, D = X.shape
    NH = Wq.shape[1] // HD
    NKV = Wk.shape[1] // HD
    REP = NH // NKV
    HID = w1.shape[0]
    NQ = T // P
    KD = D // P
    KF = HID // P
    KO = NH * HD // P
    KM = NKV * HD // P
    KEYS = P + SINK
    BLOCKS = T // WINDOW
    UNITS = NQ * NKV
    NT = B * NQ
    SCALE = 1.0 / HD ** 0.5
    assert T % P == 0 and REP == 4 and NQ == 4 and KD == 2 and P == 2 * WINDOW

    x_tiles = X.rearrange("b (n p) d -> p (b n) d", p=P)
    out_tiles = out.rearrange("b (n p) d -> p (b n) d", p=P)

    ctx = ExitStack()
    with ctx:
        def sb(name, shape, dt=F32, scope=ctx):
            return scope.enter_context(nc.sbuf_tensor(name, shape, dt))

        def sem(name):
            return ctx.enter_context(nc.semaphore(name))

        x_all = sb("x_all", [P, B * NQ, D])
        wq_hi, wq_lo = (sb(f"wq_{s}", [P, KD, NH * HD], F32R) for s in ("hi", "lo"))
        wk_hi, wk_lo = (sb(f"wk_{s}", [P, KD, NKV * HD], F32R) for s in ("hi", "lo"))
        wv_hi, wv_lo = (sb(f"wv_{s}", [P, KD, NKV * HD], F32R) for s in ("hi", "lo"))
        wo_hi, wo_lo = (sb(f"wo_{s}", [P, KO, D], F32R) for s in ("hi", "lo"))
        with ExitStack() as raw:
            w_raw = [sb(f"w_raw{i}", [P, KF * D], scope=raw)[:, :] for i in range(2)]
        t1T = sb("t1T", [P, KD, HID], F32R)
        t2T = sb("t2T", [P, KF, D], F32R)
        abs_w = sb("abs_w", [P, KF * D])
        tern = abs_w[:, :].bitcast(BF16).rearrange("p (w c) -> p w c", w=2)
        tot_row = sb("tot_row", [2, 8])
        tot = sb("tot", [2, 1])
        tot_diag = sb("tot_diag", [2, 2])
        bias1 = sb("bias1", [P, HID])
        bias2 = sb("bias2", [P, D])
        pos, neg = (bias1[:, i * HID // 2:(i + 1) * HID // 2].bitcast(BF16) for i in range(2))
        abs_64 = bias2[:, 0:128].rearrange("p (w c) -> p w c", w=2)
        abs_8 = bias2[:, 128:144].rearrange("p (w c) -> p w c", w=2)
        f_moments = sb("f_moments", [P, NT, 2])
        f_var = sb("f_var", [P, NT])
        f_r1 = sb("f_r1", [P, NT])
        scale1 = sb("scale1", [P, NT])
        x_stats = sb("x_stats", [P, B * NQ, 6])
        lnb1 = sb("lnb1", [P, KD])
        lnb2 = sb("lnb2", [P, KF])
        mask_block0 = sb("mask_block0", [P, P])
        mask_block1 = sb("mask_block1", [P, P])
        mask_rest = sb("mask_rest", [P, KEYS])
        mask_low = sb("mask_low", [P, P])
        ident = sb("ident", [P, P])
        ident_bf = sb("ident_bf", [P, P], BF16)
        ones = sb("ones", [P, P])
        neg_half = sb("neg_half", [P, B * NQ])
        wscale = sb("wscale", [P, 2])
        winv = sb("winv", [P, 2])
        gate = sb("gate", [P, 32])
        wsum = sb("wsum", [P, 2])
        wmean = sb("wmean", [P, 2])
        wscale_sq = sb("wscale_sq", [P, 2])

        setup = ExitStack()
        with setup:
            st_wq = sb("st_wq", [P, KD, NH * HD], scope=setup)
            st_wk = sb("st_wk", [P, KD, NKV * HD], scope=setup)
            st_wv = sb("st_wv", [P, KD, NKV * HD], scope=setup)
            st_wo = sb("st_wo", [P, KO, D], scope=setup)

        attn = ExitStack()
        with attn:
            y_hi, y_lo = (sb(f"y_{s}", [P, NQ, KO // 2, P], F32R, attn) for s in ("hi", "lo"))
            pt_own = sb("pt_own", [P, 2, REP * P], scope=attn)
            stats = sb("stats", [P, NQ, 6], scope=attn)
            moments = sb("moments", [P, NQ, 2], scope=attn)
            var_eps = sb("var_eps", [P, NQ], scope=attn)
            rstd = sb("rstd", [P, NQ], scope=attn)
            xt_hi, xt_lo = (sb(f"xt_{s}", [P, KD, T], F32R, attn) for s in ("hi", "lo"))
            qq = sb("qq", [P, 2, BLOCKS, REP, WINDOW], F32R, attn)
            kk_hi, kk_lo = (sb(f"kk_{s}", [P, NKV, NQ, 2, KEYS], F32R, attn) for s in ("hi", "lo"))
            v_own = sb("v_own", [P, NQ, NKV * HD], scope=attn)
            v_mid = sb("v_mid", [P, NQ - 1, NKV * HD], scope=attn)
            v_sink = sb("v_sink", [REP * SINK, NKV, REP, HD], scope=attn)
            xn = sb("xn", [P, NQ, D], scope=attn)
            probs = sb("probs", [P, 2, REP, KEYS], scope=attn)
            sink_probs = sb("sink_probs", [P, 2, REP * SINK], scope=attn)
            neg_max = sb("neg_max", [P, 2, REP], scope=attn)
            row_sum = sb("row_sum", [P, 2, REP], scope=attn)
            row_rec = sb("row_rec", [P, 4, REP], scope=attn)
            yn = sb("yn", [P, 2, REP * HD], scope=attn)
            pt_sink = sb("pt_sink", [REP * SINK, 2, P], scope=attn)

        ffn = ExitStack()
        with ffn:
            hid = sb("hid", [P, 4, HID], scope=ffn)
            h_square = sb("h_square", [P, HID], scope=ffn)
            h_sum = sb("h_sum", [P, 4], scope=ffn)
            h_sumsq = sb("h_sumsq", [P, 4], scope=ffn)
            h_negmean = sb("h_negmean", [P, 4], scope=ffn)
            h_var = sb("h_var", [P, 4], scope=ffn)
            scale2 = sb("scale2", [P, 4], scope=ffn)
            gain1 = sb("gain1", [P, D], scope=ffn)
            f_xm = sb("f_xm", [P, 2, D], scope=ffn)
            fx_hi, fx_lo = (sb(f"fx_{s}", [P, 2, D], F32R, ffn) for s in ("hi", "lo"))
            gain2 = sb("gain2", [P, HID], scope=ffn)
            f_xb = sb("f_xb", [P, 4, D], scope=ffn)
            f_out = sb("f_out", [P, 4, D], scope=ffn)
            hg = sb("hg", [P, 4, HID], scope=ffn)
            ht_hi, ht_lo = (sb(f"ht_{s}", [P, HID], F32R, ffn) for s in ("hi", "lo"))

        psum = ExitStack()
        with psum:
            ps_score = [psum.enter_context(nc.psum_tensor(f"ps_score{i}", [P, 512], F32)) for i in range(2)]
            ps_job = [psum.enter_context(nc.psum_tensor(f"ps_job{i}", [P, 512], F32)) for i in range(2)]
            ps_pt_own = psum.enter_context(nc.psum_tensor("ps_pt_own", [P, 512], F32))
            ps_pt_sink = psum.enter_context(nc.psum_tensor("ps_pt_sink", [P, 512], F32))
            ps_y = psum.enter_context(nc.psum_tensor("ps_y", [P, 512], F32))
            ps_yt = psum.enter_context(nc.psum_tensor("ps_yt", [P, 512], F32))
        psum_ffn = ExitStack()
        with psum_ffn:
            ps_z = [psum_ffn.enter_context(nc.psum_tensor(f"ps_z{i}", [P, 1024], F32)) for i in range(2)]
            ps_th = [psum_ffn.enter_context(nc.psum_tensor(f"ps_th{i}", [P, 512], F32)) for i in range(2)]
            ps_tx = psum_ffn.enter_context(nc.psum_tensor("ps_tx", [P, 512], F32))
            ps_o = psum_ffn.enter_context(nc.psum_tensor("ps_o", [P, 512], F32))

        x_loaded = sem("x_loaded")
        aw_loaded = [sem(f"aw_loaded{i}") for i in range(4)]
        w_loaded = [sem(f"w_loaded{i}") for i in range(2)]
        v_loaded = sem("v_loaded")
        pool_consts = sem("pool_consts")
        ident_ready = sem("ident_ready")
        masks_ready = sem("masks_ready")
        hi_ready = sem("hi_ready")
        lo_ready = sem("lo_ready")
        abs_ready = sem("abs_ready")
        abs_read = sem("abs_read")
        sums_ready = sem("sums_ready")
        setup_done = sem("setup_done")
        dve_step = sem("dve_step")
        tern_ready = sem("tern_ready")

        dve_chain = sem("dve_chain")
        var_ready = sem("var_ready")
        rstd_ready = sem("rstd_ready")
        xn_ready = sem("xn_ready")
        job_mm = sem("job_mm")
        job_hi = sem("job_hi")
        job_free = sem("job_free")
        keys_ready = sem("keys_ready")
        k_swapped = sem("k_swapped")
        v_moved = [sem(f"v_moved{i}") for i in range(1, NQ)]
        s_moved = sem("s_moved")
        sinks_ready = sem("sinks_ready")
        score_mm = sem("score_mm")
        score_free = sem("score_free")
        exp_done = sem("exp_done")
        rec_chain = sem("rec_chain")
        rec_ready = sem("rec_ready")
        pt_mm = sem("pt_mm")
        pt_own_done = sem("pt_own_done")
        pt_sink_done = sem("pt_sink_done")
        y_mm = sem("y_mm")
        yn_ready = sem("yn_ready")
        yt_mm = sem("yt_mm")
        y_hi_done = sem("y_hi_done")
        y_free = sem("y_free")

        ffn_loaded = sem("ffn_loaded")
        gain_loaded = [sem(f"gain_loaded{i}") for i in range(2)]
        f_chain = sem("f_chain")
        f_pow_in = sem("f_pow_in")
        f_pow_out = sem("f_pow_out")
        xm_ready = sem("xm_ready")
        xb_ready = sem("xb_ready")
        tx_mm = sem("tx_mm")
        tx_hi = sem("tx_hi")
        tx_free = sem("tx_free")
        z_mm = sem("z_mm")
        z_free = sem("z_free")
        gelu_done = sem("gelu_done")
        squares_done = sem("squares_done")
        var_done = sem("var_done")
        mean_ready = sem("mean_ready")
        centred = sem("centred")
        hn_ready = sem("hn_ready")
        scale2_ready = sem("scale2_ready")
        th_mm = sem("th_mm")
        th_hi = sem("th_hi")
        th_free = sem("th_free")
        o_mm = sem("o_mm")
        o_free = sem("o_free")
        stored = [sem(f"stored{i}") for i in range(4)]

        JOBS_AT = {0: [("V", 1, 0), ("Q", 2, 0)], 1: [("V", 2, 0), ("Q", 3, 0)], 2: [("O", 4, -1), ("V", 3, 0)],
                   3: [("O", 5, -1), ("K", 1, 0)], 4: [("O", 6, -1)], 5: [("O", 7, -1), ("Q", 4, 0), ("S", 0, 2)],
                   6: [("Q", 5, 0)], 7: [("Q", 6, 0)], 8: [("Q", 7, 0), ("S", 1, 2)],
                   9: [("X", 0, 1), ("X", 1, 1), ("T", 0, 3)], 10: [("O", 0, 0), ("T", 1, 3)],
                   11: [("O", 1, 0), ("K", 0, 1), ("T", 2, 3)], 12: [("O", 2, 0), ("Q", 0, 1), ("T", 3, 3)],
                   13: [("O", 3, 0), ("Q", 1, 1), ("B", 0, 3)], 14: [("B", 1, 3)],
                   15: [("V", 0, 1), ("B", 2, 3)]}
        ABS_STEPS, SUM_STEPS, TERN_STEPS = (0, 2), (1, 3), (9, 11, 13, 15)
        MOMENT_STEP, SCALE_STEP = 9, 12
        LN_STEP, POW_STEP, XN_STEP = 5, 6, 7
        KEY_STEPS = {5: ("K", 1, 0), 6: ("K", 1, 0), 12: ("K", 0, 1), 13: ("K", 0, 1)}
        ORDER = [j for s in range(UNITS) for j in JOBS_AT.get(s, [])]
        HI_ORDER = [j for j in ORDER if j[0] in "QXK"]
        JOBS, HIS = sum(j[2] < 2 for j in ORDER), len(HI_ORDER)
        FIRST_JOBS, LAST_JOBS = (sum(j[2] == r for j in ORDER) for r in (2, 3))
        NEXT_JOBS = sum(j[2] == 1 for j in ORDER)
        NEXT_HIS = sum(j[2] == 1 for j in HI_ORDER)
        assert JOBS % 2 == 0 and KO == 2 * NKV and NQ == NKV == 4
        PRE, FIRST, MID, LAST, DRAIN = range(5)
        ON = {-1: (MID, LAST, DRAIN), 0: (FIRST, MID, LAST), 1: (PRE, FIRST, MID),
              2: (FIRST,), 3: (LAST,)}

        def has(phase, rel):
            return phase in ON[rel]

        def at(b, per_batch, offset):
            return b[0] * per_batch + (b[1] * per_batch + offset)

        def jobs_of(phase, s):
            return [j for j in JOBS_AT.get(s, []) if has(phase, j[2])]

        def job_offset(phase, job):
            n = [j for j in ORDER if has(phase, j[2])].index(job)
            return n + (JOBS if phase == PRE else NEXT_JOBS if phase == FIRST else
                        NEXT_JOBS - NQ + FIRST_JOBS if phase in (MID, LAST) else -NQ + FIRST_JOBS + LAST_JOBS)

        def hi_offset(phase, job):
            n = [j for j in HI_ORDER if has(phase, j[2])].index(job)
            return n + (HIS if phase == PRE else NEXT_HIS)

        def job_done(phase, b, kind, i):
            job = [j for j in ORDER if j[:2] == (kind, i)][0]
            if job[2] == 1:
                before = {FIRST: PRE, MID: MID, LAST: MID}[phase]
                return at(b, JOBS, job_offset(before, job) - JOBS + 3)
            return at(b, JOBS, job_offset(phase, job) + 3)

        PAIRS = 2 * UNITS
        SINK_UNITS = UNITS - NKV
        ALL_JOBS = B * JOBS + FIRST_JOBS + LAST_JOBS

        def sink_units_before(u):
            return u - (u // NQ + 1)

        def batch_ring(eng, body, after_pre=None):
            body(PRE, (0, -1))
            if after_pre:
                after_pre()
            body(FIRST, (0, 0))
            with eng.Fori(0, B - 2) as r:
                body(MID, (r, 1))
            body(LAST, (0, B - 1))
            body(DRAIN, (0, B))

        def active(n, t):
            return not isinstance(n, int) or 0 <= t < NT

        def tile_loop(eng, step, first=-2, before_loop=None):
            for k in range(first, 3):
                step(0, k)
            if before_loop:
                before_loop()
            with eng.Fori(0, (NT - 8) // 4) as n:
                for k in range(3, 7):
                    step(n, k)
            for k in range(NT - 5, NT + 3):
                step(0, k)

        block = ctx.enter_context(nc.Block())

        @block.sync
        def _(sp):
            sp.dma_start(x_all[:, 0:NQ, :], x_tiles[:, 0:NQ, :]).then_inc(x_loaded, 16)
            with nc.allow_non_contiguous_dma(reason="per-partition vectors of the layer norms"):
                sp.dma_start(lnb1[:, :], ln1_b.rearrange("(k p) -> p k", p=P)).then_inc(v_loaded, 16)
                sp.dma_start(lnb2[:, :], ln2_b.rearrange("(k p) -> p k", p=P)).then_inc(v_loaded, 16)
            sp.wait_ge(aw_loaded[3], 64)
            sp.wait_ge(x_loaded, 32)
            sp.dma_start(x_all[:, NQ:2 * NQ, :], x_tiles[:, NQ:2 * NQ, :]).then_inc(x_loaded, 16)

            def swap_keys(phase, b, job):
                m = job[1]
                lower, upper = slice(0, HD), slice(HD, P)
                for kk in (kk_hi, kk_lo):
                    if kk is kk_hi:
                        sp.wait_ge(job_hi, at(b, HIS, hi_offset(phase, job) + 1))
                    else:
                        sp.wait_ge(job_free, at(b, JOBS, job_offset(phase, job) + 3))
                    for g, src, dst in ((2 * m, lower, upper), (2 * m + 1, upper, lower)):
                        sp.dma_start(kk[dst, g, :, 1, 0:P].bitcast(F32), kk[src, g, :, 1, 0:P].bitcast(F32))\
                          .then_inc(k_swapped, 16)

            def move_values(count, i):
                sp.wait_ge(job_free, count)
                sp.dma_start(v_mid[0:WINDOW, i - 1, :], v_own[WINDOW:P, i - 1, :]).then_inc(v_moved[i - 1], 16)
                sp.dma_start(v_mid[WINDOW:P, i - 1, :], v_own[0:WINDOW, i, :]).then_inc(v_moved[i - 1], 16)

            def move_sinks(phase, b):
                sp.wait_ge(y_mm, at(b, UNITS, 2))
                for j in range(REP):
                    sp.dma_start(v_sink[SINK * j:SINK * (j + 1), :, j, :],
                                 v_own[0:SINK, 0, :].rearrange("p (g d) -> p g d", g=NKV)).then_inc(s_moved, 16)

            def body(phase, b):
                if phase == MID:
                    sp.wait_ge(x_loaded, at(b, 16, 32))
                    rows = bass.ds(at(b, NQ, NQ), NQ)
                    sp.dma_start(x_all[:, rows, :], x_tiles[:, rows, :]).then_inc(x_loaded, 16)
                for s in range(UNITS):
                    if has(phase, 0) and s == 2:
                        move_sinks(phase, b)
                    for job in jobs_of(phase, s):
                        if job[0] == "K":
                            swap_keys(phase, b, job)
                        if job[0] == "V" and job[1]:
                            move_values(at(b, JOBS, job_offset(phase, job) + 3), job[1])

                    if phase == LAST and s == 9:
                        sp.wait_ge(job_free, job_done(phase, b, "Q", 7))
                        sp.dma_start(gain1[:, :], ln1_g.partition_broadcast(P)).then_inc(gain_loaded[0], 16)

                if phase == FIRST:
                    sp.wait_ge(tern_ready, 4)
                    for dst, src in ((bias1, b1), (bias2, b2)):
                        sp.dma_start(dst[:, :], src.partition_broadcast(P)).then_inc(ffn_loaded, 16)

            batch_ring(sp, body, lambda: sp.wait_ge(masks_ready, 1))
            sp.wait_ge(job_free, 2 + ALL_JOBS)
            sp.dma_start(gain2[:, :], ln2_g.partition_broadcast(P)).then_inc(gain_loaded[1], 16)
            with sp.Fori(0, B) as c:
                for j in range(4):
                    sp.wait_ge(o_free, c * 4 + (1 + j + 1))
                    sp.dma_start(out_tiles[:, bass.ds(c * 4 + j, 1), :], f_out[:, j:j + 1, :])\
                      .then_inc(stored[j], 16)
            for j in range(4):
                sp.wait_ge(stored[j], 16 + 16 * B)

        @block.gpsimd
        def _(pool):
            def pool_gate():
                pool.tensor_tensor(gate[:, 0:1], ones[:, 0:1], ones[:, 0:1], ALU.mult)

            n = [0]

            def link(ins):
                n[0] += 1
                ins.then_inc(pool_consts, 1)
                pool.wait_ge(pool_consts, n[0])

            pool.memset(ones[:, :], 1.0)
            pool.memset(neg_half[:, :], -0.5)
            for m in (ident, ident_bf):
                link(pool.memset(m[:, :], 0.0))
                link(pool.affine_select(out=m[:, :], in_=m[:, :], compare_op=ALU.not_equal, fill=1.0,
                                        base=0, pattern=[[-1, P]], channel_multiplier=1))
            pool.memset(gate[:, 30:31], 0.0).then_inc(ident_ready, 1)

            def build_masks():
                for m, block in ((mask_block0, 0), (mask_block1, 1), (mask_rest, 2)):
                    for dst, first in ((m, 0), (mask_low, WINDOW)):
                        link(pool.memset(dst[:, :], 0.0))
                        if block == 0:
                            link(pool.affine_select(out=dst[:, 0:P], in_=dst[:, 0:P], compare_op=ALU.is_ge, fill=MASKED,
                                                    base=-first, pattern=[[-1, P]], channel_multiplier=1))
                            continue
                        link(pool.affine_select(out=dst[:, 0:P], in_=dst[:, 0:P], compare_op=ALU.is_ge, fill=MASKED,
                                                base=WINDOW - first, pattern=[[-1, P]], channel_multiplier=1))
                        lo = SINK if block == 1 else 0
                        link(pool.affine_select(out=dst[:, lo:P], in_=dst[:, lo:P], compare_op=ALU.is_ge, fill=MASKED,
                                                base=lo - 1 + first, pattern=[[1, P - lo]], channel_multiplier=-1))
                    link(pool.tensor_copy(m[WINDOW:P, 0:P], mask_low[WINDOW:P, :]))
                pool.memset(v_sink[:, :, :, :], 0.0)
                pool.memset(gate[:, 31:32], 0.0).then_inc(masks_ready, 1)

            def power(b):
                pool.wait_ge(var_ready, at(b, 1, 2))
                pool.tensor_tensor(rstd[:, :], var_eps[:, :], neg_half[:, 0:NQ], ALU.pow).then_inc(rstd_ready, 1)

            def scale_power(lo, hi, n):
                pool.wait_ge(f_pow_in, n)
                pool.tensor_tensor(f_r1[:, lo:hi], f_var[:, lo:hi], neg_half[:, lo:hi], ALU.pow).then_inc(f_pow_out, 1)

            def key_columns(count, m, lo):
                if not lo:
                    pool.wait_ge(k_swapped, count)
                    pool_gate()
                g, rest = slice(2 * m, 2 * m + 2), slice(1, NQ)
                kk = kk_lo if lo else kk_hi
                pool.tensor_copy(kk[:, g, rest, 0, 0:WINDOW], kk[:, g, 0:NQ - 1, 1, WINDOW:P])
                pool.tensor_copy(kk[:, g, rest, 0, WINDOW:P], kk[:, g, rest, 1, 0:WINDOW])
                for block in range(2):
                    last = pool.tensor_copy(kk[:, g, rest, block, P:KEYS],
                                            kk[:, g, 0:1, 1, 0:SINK].to_broadcast([P, 2, NQ - 1, SINK]))
                last.then_inc(keys_ready, 1)

            def gather_sinks(b, u):
                pool.wait_ge(exp_done, at(b, UNITS, 2 + u + 1))
                pool.tensor_tensor(sink_probs[:, u % 2, :].rearrange("p (j s) -> p j s", j=REP),
                                   probs[:, u % 2, :, P:KEYS], ones[:, 0:REP * SINK].rearrange("p (j s) -> p j s", j=REP),
                                   ALU.mult).then_inc(sinks_ready, 1)

            def body(phase, b):
                for s in range(UNITS):
                    if has(phase, 0) and s % NQ:
                        gather_sinks(b, s)
                    if s in KEY_STEPS and has(phase, KEY_STEPS[s][2]):
                        m = KEY_STEPS[s][1]
                        key_columns(at(b, 64 * KM, 64 * KM if m else 64 * KM + 64), m, s - 1 in KEY_STEPS)
                    if has(phase, 1) and s == POW_STEP:
                        power(b)
                        if phase == PRE:
                            build_masks()
                    if phase == LAST and s == MOMENT_STEP + 1:
                        scale_power(0, NT - NQ, 1)

            batch_ring(pool, body)

            scale_power(NT - NQ, NT, 2)
            pool.wait_ge(gain_loaded[1], 16)

            def step(n, k):
                t = k - 1
                if active(n, t):
                    pool.wait_ge(centred, n * 4 + (t + 1))
                    pool.tensor_tensor(hg[:, t % 4, :], hid[:, t % 4, :], gain2[:, :], ALU.mult).then_inc(hn_ready, 1)
                    pool.tensor_tensor(f_xb[:, t % 4:t % 4 + 1, :], x_all[:, bass.ds(n * 4 + t, 1), :],
                                       bias2[:, :].unsqueeze(1), ALU.add).then_inc(xb_ready, 1)
                    pool.wait_ge(var_done, n * 4 + (t + 1))
                    pool.tensor_tensor(scale2[:, t % 4:t % 4 + 1], h_var[:, t % 4:t % 4 + 1], neg_half[:, 0:1],
                                       ALU.pow).then_inc(scale2_ready, 1)

            tile_loop(pool, step)

        @block.scalar
        def _(act):
            loads = ((st_wk, Wk), (st_wq, Wq), (st_wv, Wv), (st_wo, Wo))
            for i, (dst, src) in enumerate(loads[:3]):
                act.dma_start(dst[:, :, :], src.rearrange("(k p) n -> p k n", p=P)).then_inc(aw_loaded[i], 16)
            for pair in range(2):
                for h in range(2):
                    act.dma_start(st_wo[pair * HD:(pair + 1) * HD, :, :].rearrange("p (g h) n -> p g h n", g=NKV)[:, :, h, :],
                                  Wo.rearrange("(g a h d) n -> a h d g n", g=NKV, a=2, h=2)[pair, h]).then_inc(aw_loaded[3], 16)
            act.dma_start(w_raw[0].rearrange("p (n d) -> p n d", n=KF), w1.rearrange("(n p) d -> p n d", p=P))\
               .then_inc(w_loaded[0], 16)
            act.dma_start(w_raw[1].rearrange("p (n h) -> p n h", n=KD), w2.rearrange("(n p) h -> p n h", p=P))\
               .then_inc(w_loaded[1], 16)

            def weight_hi_part(i):
                hi, src = ((wk_hi, st_wk), (wq_hi, st_wq), (wv_hi, st_wv), (wo_hi, st_wo))[i]
                act.wait_ge(aw_loaded[i], 64 if i == 3 else 16)
                act.activation(hi[:, :, :], src[:, :, :], ACT.Copy).then_inc(hi_ready, 1)

            weight_hi_part(0)

            def hi_part(phase, b, job):
                kind, i, _ = job
                offset = job_offset(phase, job)
                ps = ps_job[offset % 2]
                act.wait_ge(job_mm, at(b, JOBS, offset + 1))
                if kind == "X":
                    act.activation(xt_hi[:, i, :], ps[:, :], ACT.Copy).then_inc(job_hi, 1)
                    return
                for half in range(2):
                    rows = slice(half * HD, (half + 1) * HD)
                    if kind == "K":
                        last = act.activation(kk_hi[rows, 2 * i + half, :, 1, 0:P],
                                              ps[rows, :].rearrange("p (n t) -> p n t", n=NQ), ACT.Copy)
                    else:
                        last = act.activation(qq[rows, i // 2 % 2, :, i % 2 * 2 + half, :],
                                              ps[rows, :].rearrange("p (n t) -> p n t", n=BLOCKS), ACT.Copy, scale=SCALE)
                last.then_inc(job_hi, 1)

            def exps(b, u):
                w = KEYS if u % NQ else P
                act.wait_ge(rec_ready, at(b, UNITS, u + 1))
                for j in range(REP):
                    if j % 2 == 0:
                        act.wait_ge(score_free, at(b, PAIRS, 2 + 2 * u + j // 2 + 1))
                    last = act.activation(probs[:, u % 2, j, 0:w], probs[:, u % 2, j, 0:w], ACT.Exp,
                                          bias=neg_max[:, u % 2, j:j + 1], scale=-1.0,
                                          accum_out=row_sum[:, u % 2, j:j + 1])
                last.then_inc(exp_done, 1)

            def copy_pt(b, u):
                act.wait_ge(pt_mm, at(b, UNITS, 4 + u + 1))
                act.wait_ge(y_mm, at(b, UNITS, u + 1))
                act.activation(pt_own[:, u % 2, :], ps_pt_own[:, :], ACT.Copy).then_inc(pt_own_done, 1)

            def y_hi_part(phase, b, u):
                g, qb = divmod(u % UNITS, NQ)
                act.wait_ge(yt_mm, at(b, UNITS, 2 + u + 1))
                if 0 <= u < NQ and has(phase, -1):
                    act.wait_ge(job_mm, at(b, JOBS, job_offset(phase, ("O", NQ + qb, -1)) + 1))
                elif u >= 0 and g == 2:
                    act.wait_ge(job_mm, at(b, JOBS, job_offset(phase, ("O", qb, 0)) + 1))
                act.activation(y_hi[:, qb, g % 2 * 2:g % 2 * 2 + 2, :].rearrange("p h (b t) -> p h b t", b=2),
                               ps_yt[:, 0:2 * P].rearrange("p (b h t) -> p h b t", b=2, h=2), ACT.Copy)\
                   .then_inc(y_hi_done, 1)

            def body(phase, b):
                for s in range(UNITS):
                    if phase == FIRST and s == 2:
                        act.wait_ge(setup_done, 1)
                    if has(phase, 0 if s >= 2 else -1):
                        copy_pt(b, s - 2)
                    if has(phase, 0):
                        exps(b, s)
                    if has(phase, 0 if s >= 4 else -1):
                        y_hi_part(phase, b, s - 4)
                    for job in jobs_of(phase, s):
                        if job in HI_ORDER:
                            hi_part(phase, b, job)
                    if phase == PRE and s == 10:
                        weight_hi_part(1)
                        weight_hi_part(2)
                    if phase == FIRST and s in ABS_STEPS:
                        i = ABS_STEPS.index(s)
                        act.wait_ge(w_loaded[i], 16)
                        if i:
                            act.wait_ge(abs_read, 1)
                        act.activation(abs_w[:, :], w_raw[i], ACT.Abs).then_inc(abs_ready, 1)

            batch_ring(act, body, lambda: weight_hi_part(3))

            def step(n, k):
                t = k - 3
                if active(n, t):
                    for h in range(2):
                        act.wait_ge(th_mm, n * 8 + (2 * t + h + 1))
                        act.activation(ht_hi[:, 512 * h:512 * h + 512], ps_th[h][:, :], ACT.Copy).then_inc(th_hi, 1)
                t = k - 1
                if active(n, t):
                    act.wait_ge(mean_ready, n * 4 + (t + 1))
                    act.activation(hid[:, t % 4, :], hid[:, t % 4, :], ACT.Identity,
                                   bias=h_negmean[:, t % 4:t % 4 + 1]).then_inc(centred, 1)
                    act.wait_ge(centred, n * 4 + (t + 1))
                    act.activation(h_square[:, :], hid[:, t % 4, :], ACT.Square,
                                   accum_out=h_sumsq[:, t % 4:t % 4 + 1]).then_inc(squares_done, 1)
                t = k + 1
                if active(n, t):
                    act.wait_ge(tx_mm, n * 4 + (t + 1))
                    act.activation(fx_hi[:, t % 2, :], ps_tx[:, 0:D], ACT.Copy).then_inc(tx_hi, 1)
                t = k
                if active(n, t):
                    act.wait_ge(z_free, n * 4 + (2 + t + 1))
                    act.activation(hid[:, t % 4, :], hid[:, t % 4, :], ACT.Gelu,
                                   accum_out=h_sum[:, t % 4:t % 4 + 1]).then_inc(gelu_done, 1)

            tile_loop(act, step)

        @block.vector
        def _(dve):
            def dve_gate(i=0):
                dve.memset(gate[:, 1 + i:2 + i], 0.0)

            for i, (s, n) in enumerate(((job_free, 2), (score_free, 2), (exp_done, 2), (rec_ready, 2), (yn_ready, 4), (yt_mm, 2),
                         (pt_mm, 4), (pt_own_done, 1), (pt_sink_done, 1), (y_mm, 2), (y_free, 1),
                         (tx_free, 1), (th_free, 2), (z_free, 2), (o_free, 1), (x_loaded, 16),
                         *((x, 16) for x in stored))):
                dve.memset(gate[:, 8 + i:9 + i], 0.0).then_inc(s, n)
            steps = [0]

            def link(ins):
                steps[0] += 1
                ins.then_inc(dve_step, 1)
                dve.wait_ge(dve_step, steps[0])

            def weight_lo_part(i):
                lo, hi, src = ((wk_lo, wk_hi, st_wk), (wq_lo, wq_hi, st_wq), (wv_lo, wv_hi, st_wv),
                               (wo_lo, wo_hi, st_wo))[i]
                dve.wait_ge(hi_ready, i + 1)
                ins = dve.tensor_tensor(lo[:, :, :], src[:, :, :], hi[:, :, :].bitcast(F32), ALU.subtract)
                ins.then_inc(lo_ready, 1)

            def abs_sums(i):
                dve.wait_ge(abs_ready, i + 1)
                dve.tensor_reduce(abs_64[:, i, :], abs_w[:, :].rearrange("p (a c) -> p a c", a=64), AX_X, ALU.add)\
                   .then_inc(abs_read, 1)
                dve.wait_ge(abs_read, i + 1)
                link(dve.tensor_reduce(abs_8[:, i, :], abs_64[:, i, :].rearrange("p (a c) -> p a c", a=8), AX_X, ALU.add))
                if i:
                    dve.tensor_reduce(wsum[:, :], abs_8[:, :, :], AX_X, ALU.add).then_inc(sums_ready, 1)

            def ternary(i, half):
                cols = slice(half * KF * D // 2, (half + 1) * KF * D // 2)
                link(dve.tensor_scalar(pos[:, :], w_raw[i][:, cols], wscale[:, i:i + 1], 0.5, ALU.mult, ALU.is_gt))
                link(dve.tensor_scalar(neg[:, :], w_raw[i][:, cols], wscale[:, i:i + 1], -0.5, ALU.mult, ALU.is_lt))
                dve.tensor_tensor(tern[:, i, cols], pos[:, :], neg[:, :], ALU.subtract).then_inc(tern_ready, 1)
                dve.wait_ge(tern_ready, 2 * i + half + 1)

            def lo_part(phase, b, job):
                kind, i, _ = job
                offset = job_offset(phase, job)
                ps = ps_job[offset % 2]
                if job in HI_ORDER:
                    dve.wait_ge(job_hi, at(b, HIS, hi_offset(phase, job) + 1))
                else:
                    dve.wait_ge(job_mm, at(b, JOBS, offset + 1))
                if kind == "X":
                    ins = dve.tensor_tensor(xt_lo[:, i, :], ps[:, :], xt_hi[:, i, :].bitcast(F32), ALU.subtract)
                elif kind in "KQ":
                    for half in range(2):
                        rows, other = slice(half * HD, (half + 1) * HD), slice((1 - half) * HD, (2 - half) * HD)
                        if kind == "K":
                            ins = dve.tensor_tensor(kk_lo[rows, 2 * i + half, :, 1, 0:P],
                                                    ps[rows, :].rearrange("p (n t) -> p n t", n=NQ),
                                                    kk_hi[rows, 2 * i + half, :, 1, 0:P].bitcast(F32), ALU.subtract)
                        else:
                            slot, j = i // 2 % 2, i % 2 * 2 + half
                            ins = dve.scalar_tensor_tensor(out=qq[other, slot, :, j, :],
                                                           in0=ps[rows, :].rearrange("p (n t) -> p n t", n=BLOCKS),
                                                           scalar=SCALE, in1=qq[rows, slot, :, j, :].bitcast(F32),
                                                           op0=ALU.mult, op1=ALU.subtract)
                elif kind == "S" and i == 0:
                    link(dve.tensor_reduce(tot_row[:, :], ps[0:2, 0:P].rearrange("w (a c) -> w a c", a=8), AX_X, ALU.add))
                    link(dve.tensor_reduce(tot[:, :], tot_row[:, :], AX_X, ALU.add))
                    dve.tensor_scalar(tot_diag[:, :], ident[0:2, 0:2], tot[:, 0:1], None, ALU.mult)\
                       .then_inc(sums_ready, 1)
                    ins = dve.memset(gate[:, 7:8], 0.0)
                elif kind == "S":
                    link(dve.tensor_scalar(wmean[:, :], ps[:, 0:2], 1.0 / (HID * D), 1e-5, ALU.mult, ALU.max))
                    link(dve.reciprocal(wscale[:, :], wmean[:, :]))
                    link(dve.reciprocal(winv[:, :], wscale[:, :]))
                    link(dve.tensor_tensor(wscale_sq[:, :], wscale[:, :], wscale[:, :], ALU.mult))
                    ins = dve.tensor_scalar(wscale_sq[:, :], wscale_sq[:, :], 1.0 / HID, None, ALU.mult)
                elif kind == "T":
                    ins = dve.tensor_copy((t1T, t2T)[i // 2][:, :, :].rearrange("p a c -> p (a c)")
                                          [:, i % 2 * HID:(i % 2 + 1) * HID], ps[:, :].bitcast(BF16))
                elif kind == "B":
                    dve.wait_ge(ffn_loaded, 32)
                    dst = bias2[:, :] if i == 2 else bias1[:, 512 * i:512 * i + 512]
                    ins = dve.scalar_tensor_tensor(out=dst, in0=ps[:, 0:D if i == 2 else 512],
                                                   scalar=winv[:, i // 2:i // 2 + 1], in1=dst,
                                                   op0=ALU.mult, op1=ALU.add)
                elif kind == "V":
                    ins = dve.tensor_copy(v_own[:, i, :], ps[:, 0:NKV * HD])
                else:
                    row = x_all[:, bass.ds(at(b, NQ, i if i < NQ else i - 2 * NQ), 1), :].rearrange("p o d -> p (o d)")
                    ins = dve.tensor_tensor(row, row, ps[:, 0:D], ALU.add)
                ins.then_inc(job_free, 1)

            def result_stats(phase, b, qb):
                dve.wait_ge(job_free, at(b, JOBS, job_offset(phase, ("O", NQ + qb, -1)) + 3))
                row = x_all[:, bass.ds(at(b, NQ, qb - NQ), 1), :].rearrange("p o d -> p (o d)")
                dve.bn_stats(x_stats[:, bass.ds(at(b, NQ, qb - NQ), 1), :].rearrange("p o s -> p (o s)"), row)

            def mask_and_max(b, u, block):
                qb = u % NQ
                w = KEYS if qb else P
                mask = mask_rest if qb else (mask_block0, mask_block1)[block]
                if block == 0:
                    dve.wait_ge(exp_done, at(b, UNITS, u + 1))
                    dve.wait_ge(pt_mm, at(b, UNITS, 4 + u - 2 + 1))
                dve.wait_ge(score_mm, at(b, PAIRS, 2 * u + block + 1))
                dve_gate(1 + (2 * u + block) % 4)
                for pair in range(2):
                    group = 2 * block + pair
                    last = dve.tensor_tensor_reduce(
                        probs[:, u % 2, group, 0:w], ps_score[block][:, pair * 256:pair * 256 + w],
                        mask[:, 0:w], -1.0, BIG, ALU.add, ALU.min, neg_max[:, u % 2, group:group + 1])
                last.then_inc(score_free, 1)

            def reciprocals(b, u):
                dve.wait_ge(exp_done, at(b, UNITS, 2 + u + 1))
                dve.wait_ge(yn_ready, at(b, UNITS, u + 1))
                dve.tensor_scalar(row_rec[:, u % 4, :], row_sum[:, u % 2, :], TINY, None, ALU.max)\
                    .then_inc(rec_chain, 1)
                dve.wait_ge(rec_chain, at(b, UNITS, u + 1))
                dve.reciprocal(row_rec[:, u % 4, :], row_rec[:, u % 4, :]).then_inc(rec_ready, 1)

            def copy_pt(b, u):
                dve.wait_ge(pt_mm, at(b, UNITS, 4 + u + 1))
                dve.wait_ge(y_mm, at(b, UNITS, u + 1))
                dve.tensor_copy(pt_sink[:, u % 2, :], ps_pt_sink[0:REP * SINK, 0:P]).then_inc(pt_sink_done, 1)

            def normalise_outputs(b, u):
                dve.wait_ge(y_mm, at(b, UNITS, 2 + u + 1))
                dve.wait_ge(rec_ready, at(b, UNITS, 2 + u + 1))
                dve.wait_ge(yt_mm, at(b, UNITS, u + 1))
                dve.tensor_tensor(yn[:, u % 2, :].rearrange("p (j d) -> p j d", j=REP),
                                   ps_y[:, 0:REP * HD].rearrange("p (j d) -> p j d", j=REP),
                                   row_rec[:, u % 4, :].unsqueeze(2).to_broadcast([P, REP, HD]), ALU.mult)\
                    .then_inc(yn_ready, 1)

            def y_lo_part(b, u):
                g, qb = divmod(u % UNITS, NQ)
                dve.wait_ge(y_hi_done, at(b, UNITS, u + 1))
                lo, hi = (y[:, qb, g % 2 * 2:g % 2 * 2 + 2, :].rearrange("p h (b t) -> p h b t", b=2)
                          for y in (y_lo, y_hi))
                dve.tensor_tensor(lo, ps_yt[:, 0:2 * P].rearrange("p (b h t) -> p h b t", b=2, h=2),
                                  hi.bitcast(F32), ALU.subtract).then_inc(y_free, 1)

            CHAIN = 2

            def token_stats(b):
                dve.wait_ge(x_loaded, at(b, 16, 48))
                for n in range(NQ):
                    row = x_all[:, bass.ds(at(b, NQ, NQ + n), 1), :].rearrange("p o d -> p (o d)")
                    last = dve.bn_stats(stats[:, n, :], row)
                last.then_inc(dve_chain, 1)
                dve.wait_ge(dve_chain, at(b, CHAIN, CHAIN + 1))
                dve_gate()
                for n in range(NQ):
                    last = dve.bn_aggr(moments[:, n, :], stats[:, n, :])
                last.then_inc(dve_chain, 1)
                dve.wait_ge(dve_chain, at(b, CHAIN, CHAIN + 2))
                dve.tensor_scalar(var_eps[:, :], moments[:, :, 1], LN_EPS, None, ALU.add).then_inc(var_ready, 1)

            def normalise(b):
                dve.wait_ge(rstd_ready, at(b, 1, 2))
                for n in range(NQ):
                    row = x_all[:, bass.ds(at(b, NQ, NQ + n), 1), :].rearrange("p o d -> p (o d)")
                    last = dve.tensor_scalar(xn[:, n, :], row, moments[:, n, 0:1], rstd[:, n:n + 1],
                                             ALU.subtract, ALU.mult)
                last.then_inc(xn_ready, 1)

            links = [0]

            def step_link(ins):
                links[0] += 1
                ins.then_inc(f_chain, 1)
                dve.wait_ge(f_chain, links[0])

            def moments_of(lo, hi):
                step_link(dve.memset(gate[:, 6:7], 0.0))
                for t in range(lo, hi):
                    last = dve.bn_aggr(f_moments[:, t, :], x_stats[:, t, :])
                step_link(last)
                dve.tensor_scalar(f_var[:, lo:hi], f_moments[:, lo:hi, 1], 1.0 + LN_EPS, LN_EPS * LN_EPS,
                                  ALU.mult, ALU.add).then_inc(f_pow_in, 1)

            def scales_of(lo, hi, n):
                dve.wait_ge(f_pow_out, n)
                step_link(dve.tensor_scalar(scale1[:, lo:hi], f_r1[:, lo:hi], winv[:, 0:1], None, ALU.mult))

            def body(phase, b):
                for s in range(UNITS):
                    if has(phase, 0 if s >= 1 else -1):
                        reciprocals(b, s - 1)
                    if (s - 2) % NQ and has(phase, 0 if s >= 2 else -1):
                        copy_pt(b, s - 2)
                    if has(phase, 0 if s >= 5 else -1):
                        y_lo_part(b, s - 5)
                    if has(phase, 0):
                        mask_and_max(b, s, 0)
                        mask_and_max(b, s, 1)
                    for job in jobs_of(phase, s - 1):
                        lo_part(phase, b, job)
                    if has(phase, 0 if s >= 3 else -1):
                        normalise_outputs(b, s - 3)
                    for kind, i, _ in jobs_of(phase, s - 2):
                        if kind == "O" and i >= NQ:
                            result_stats(phase, b, i - NQ)
                    if has(phase, 1) and s == LN_STEP:
                        token_stats(b)
                    if has(phase, 1) and s == XN_STEP:
                        normalise(b)
                    if phase == PRE and s == XN_STEP:
                        weight_lo_part(0)
                    if phase == PRE and s == 10:
                        weight_lo_part(1)
                        weight_lo_part(2)
                    if phase == FIRST and s in SUM_STEPS:
                        abs_sums(SUM_STEPS.index(s))
                    if phase == FIRST and s in TERN_STEPS:
                        ternary(*divmod(TERN_STEPS.index(s), 2))
                    if phase == LAST and s == MOMENT_STEP:
                        moments_of(0, NT - NQ)
                    if phase == LAST and s == SCALE_STEP:
                        scales_of(0, NT - NQ, 1)
                    if phase == DRAIN and s == 4:
                        dve.wait_ge(gain_loaded[0], 16)
                        step(0, -2)
                    if phase == DRAIN and s == 5:
                        step(0, -1)
                for job in jobs_of(phase, UNITS - 1):
                    lo_part(phase, b, job)

            def after_pre():
                weight_lo_part(3)
                dve.memset(gate[:, 5:6], 0.0).then_inc(setup_done, 1)
                dve.wait_ge(setup_done, 1)
                dve.wait_ge(masks_ready, 1)

            def step(n, k):
                t = k - 1
                if active(n, t):
                    dve.wait_ge(gelu_done, n * 4 + (t + 1))
                    dve.tensor_scalar(h_negmean[:, t % 4:t % 4 + 1], h_sum[:, t % 4:t % 4 + 1], -1.0 / HID, None,
                                      ALU.mult).then_inc(mean_ready, 1)
                t = k - 3
                if active(n, t):
                    for h in range(2):
                        dve.wait_ge(th_hi, n * 8 + (2 * t + h + 1))
                        dve.tensor_tensor(ht_lo[:, 512 * h:512 * h + 512], ps_th[h][:, :],
                                          ht_hi[:, 512 * h:512 * h + 512].bitcast(F32), ALU.subtract)\
                            .then_inc(th_free, 1)
                t = k
                if active(n, t):
                    dve.wait_ge(z_mm, n * 4 + (t + 1))
                    dve.scalar_tensor_tensor(out=hid[:, t % 4, :], in0=ps_z[t % 2][:, :],
                                             scalar=scale1[:, bass.ds(n * 4 + t, 1)], in1=bias1[:, :],
                                             op0=ALU.mult, op1=ALU.add).then_inc(z_free, 1)
                t = k + 1
                if active(n, t):
                    dve.wait_ge(tx_hi, n * 4 + (t + 1))
                    dve.tensor_tensor(fx_lo[:, t % 2, :], ps_tx[:, 0:D], fx_hi[:, t % 2, :].bitcast(F32),
                                      ALU.subtract).then_inc(tx_free, 1)
                t = k - 1
                if active(n, t):
                    dve.wait_ge(squares_done, n * 4 + (t + 1))
                    dve.tensor_scalar(h_var[:, t % 4:t % 4 + 1], h_sumsq[:, t % 4:t % 4 + 1], LN_EPS * HID,
                                      wscale_sq[:, 1:2], ALU.add, ALU.mult).then_inc(var_done, 1)
                t = k - 3
                if active(n, t):
                    dve.wait_ge(o_mm, n * 4 + (t + 1))
                    dve.wait_ge(scale2_ready, n * 4 + (t + 1))
                    dve.wait_ge(xb_ready, n * 4 + (t + 1))
                    dve.wait_ge(stored[t % 4], n * 16 + (16 + 16 * (t // 4)))
                    dve.scalar_tensor_tensor(out=f_out[:, t % 4, :], in0=ps_o[:, 0:D],
                                             scalar=scale2[:, t % 4:t % 4 + 1], in1=f_xb[:, t % 4, :],
                                             op0=ALU.mult, op1=ALU.add).then_inc(o_free, 1)
                t = k + 2
                if active(n, t):
                    row = x_all[:, bass.ds(n * 4 + t, 1), :].rearrange("p o d -> p (o d)")
                    dve.scalar_tensor_tensor(out=f_xm[:, t % 2, :], in0=row,
                                             scalar=f_moments[:, bass.ds(n * 4 + t, 1), 0:1].rearrange("p o d -> p (o d)"),
                                             in1=gain1[:, :], op0=ALU.subtract, op1=ALU.mult).then_inc(xm_ready, 1)

            batch_ring(dve, body, after_pre)
            dve.wait_ge(job_free, 2 + ALL_JOBS)
            moments_of(NT - NQ, NT)
            tile_loop(dve, step, 0, lambda: scales_of(NT - NQ, NT, 2))

        @block.tensor
        def _(pe):
            pe.wait_ge(ident_ready, 1)

            def split_matmul(dst, terms):
                n = len(terms)
                for i, (s_hi, s_lo, m_hi, m_lo) in enumerate(terms):
                    pe.matmul(dst, s_hi, m_hi, start=(i == 0), stop=False)
                    pe.matmul(dst, s_hi, m_lo, start=False, stop=False)
                    last = pe.matmul(dst, s_lo, m_hi, start=False, stop=(i == n - 1))
                return last

            def scores_of(phase, b, u, block):
                g, qb = divmod(u, NQ)
                w = KEYS if qb else P
                pe.wait_ge(score_free, at(b, PAIRS, 2 * u + block + 1))
                if block == 0 and qb == 0:
                    pe.wait_ge(job_free, job_done(phase, b, "Q", 2 * g + 1))
                    if g % 2 == 0:
                        pe.wait_ge(k_swapped, at(b, 64 * KM, 64 * (g // 2 + 1)))
                if block == 0 and qb == 1 and g % 2 == 0:
                    pe.wait_ge(keys_ready, at(b, 2 * KM, 2 * (g // 2 + 1)))
                for pair in range(2):
                    dst = ps_score[block][:, pair * 256:pair * 256 + w]
                    q = qq[:, g % 2, 2 * qb + block, 2 * pair:2 * pair + 2, :].rearrange("p j t -> p (j t)")
                    keys = 1 if qb == 0 else block
                    pe.matmul(dst, q, kk_hi[:, g, qb, keys, 0:w], start=True, stop=False)
                    last = pe.matmul(dst, q, kk_lo[:, g, qb, keys, 0:w], start=False, stop=True)
                last.then_inc(score_mm, 1)

            def transpose_probs(b, u):
                pe.wait_ge(exp_done, at(b, UNITS, 2 + u + 1))
                pe.wait_ge(pt_own_done, at(b, UNITS, u + 1))
                if u % NQ:
                    pe.wait_ge(sinks_ready, at(b, SINK_UNITS, sink_units_before(u) + 1))
                    pe.wait_ge(pt_sink_done, at(b, SINK_UNITS, sink_units_before(u) + 1))
                for j in range(REP):
                    last = pe.transpose(ps_pt_own[:, j * P:(j + 1) * P], probs[:, u % 2, j, 0:P], ident[:, :])
                if u % NQ:
                    last = pe.transpose(ps_pt_sink[0:REP * SINK, 0:P], sink_probs[:, u % 2, :], ident[:, :])
                last.then_inc(pt_mm, 1)

            def outputs_of(phase, b, u):
                g, qb = divmod(u % UNITS, NQ)
                pe.wait_ge(pt_own_done, at(b, UNITS, 1 + u + 1))
                if qb:
                    pe.wait_ge(pt_sink_done, at(b, SINK_UNITS, 1 + sink_units_before(u) + 1))
                pe.wait_ge(yn_ready, at(b, UNITS, 4 + u))
                if 0 <= u < NQ:
                    pe.wait_ge(job_free, job_done(phase, b, "V", qb))
                    if qb:
                        pe.wait_ge(v_moved[qb - 1], at(b, 32, 32))
                        pe.wait_ge(s_moved, at(b, 16 * REP, 16 * REP))
                if qb:
                    pe.matmul(ps_y[:, 0:REP * HD], pt_sink[:, u % 2, :],
                              v_sink[:, g, :, :].rearrange("p j d -> p (j d)"), start=True, stop=False)
                for j in range(REP):
                    v = v_mid[:, qb - 1, :] if qb and j < 2 else v_own[:, qb, :]
                    last = pe.matmul(ps_y[:, j * HD:(j + 1) * HD], pt_own[:, u % 2, j * P:(j + 1) * P],
                                     v[:, g * HD:(g + 1) * HD], start=(qb == 0), stop=(qb == 0 or j == REP - 1))
                last.then_inc(y_mm, 1)

            def transpose_outputs(b, u):
                pe.wait_ge(yn_ready, at(b, UNITS, 4 + u + 1))
                pe.wait_ge(y_free, at(b, UNITS, u + 1))
                for k in range(2):
                    last = pe.transpose(ps_yt[:, k * P:(k + 1) * P], yn[:, u % 2, k * P:(k + 1) * P], ident[:, :])
                last.then_inc(yt_mm, 1)

            def job_product(phase, b, job):
                kind, i, _ = job
                offset = job_offset(phase, job)
                ps = ps_job[offset % 2]
                pe.wait_ge(job_free, at(b, JOBS, offset + 1))
                if phase == PRE and kind in "KQV" or phase == FIRST and (kind, i) == ("O", 0):
                    pe.wait_ge(lo_ready, 1 + "KQVO".index(kind))
                if kind == "X":
                    pe.wait_ge(xn_ready, at(b, 1, 2))
                    for n in range(NQ):
                        last = pe.transpose(ps[:, n * P:(n + 1) * P], xn[:, n, i * P:(i + 1) * P], ident[:, :])
                elif kind == "K":
                    if i == 0:
                        pe.wait_ge(job_free, at(b, JOBS, job_offset(phase, ("X", KD - 1, 1)) + 3))
                    last = split_matmul(ps[:, :],
                                        [(wk_hi[:, k, i * P:(i + 1) * P], wk_lo[:, k, i * P:(i + 1) * P],
                                          xt_hi[:, k, :], xt_lo[:, k, :]) for k in range(KD)])
                elif kind == "V":
                    last = split_matmul(ps[:, 0:256],
                                        [(xt_hi[:, k, i * P:(i + 1) * P], xt_lo[:, k, i * P:(i + 1) * P],
                                          wv_hi[:, k, :], wv_lo[:, k, :]) for k in range(KD)])
                elif kind == "Q":
                    last = split_matmul(ps[:, :],
                                        [(wq_hi[:, k, i * P:(i + 1) * P], wq_lo[:, k, i * P:(i + 1) * P],
                                          xt_hi[:, k, :], xt_lo[:, k, :]) for k in range(KD)])
                elif kind == "S" and i == 0:
                    pe.wait_ge(sums_ready, 1)
                    last = pe.transpose(ps[0:2, 0:P], wsum[:, :], ident[:, :])
                elif kind == "S":
                    pe.wait_ge(sums_ready, 2)
                    last = pe.matmul(ps[:, 0:2], ones[0:2, :], tot_diag[:, :], start=True, stop=True)
                elif kind == "T":
                    pe.wait_ge(tern_ready, 4)
                    for n in range(KF):
                        if i < 2:
                            src = tern[:, 0, n * D + i * P:n * D + (i + 1) * P]
                        else:
                            k, d = (i - 2) * (KF // 2) + n // 2, n % 2
                            src = tern[:, 1, d * HID + k * P:d * HID + (k + 1) * P]
                        last = pe.transpose(ps[:, :].bitcast(BF16)[:, n * P:(n + 1) * P], src, ident_bf[:, :])
                elif kind == "B":
                    pe.wait_ge(v_loaded, 32)
                    pe.wait_ge(job_free, at(b, JOBS, job_offset(phase, ("T", 3 if i == 2 else 1, 3)) + 3))
                    lnb, cols = (lnb2, slice(0, D)) if i == 2 else (lnb1, slice(512 * i, 512 * i + 512))
                    w, tiles = (t2T, KF) if i == 2 else (t1T, KD)
                    for k in range(tiles):
                        last = pe.matmul(ps[:, 0:cols.stop - cols.start], lnb[:, k:k + 1].to_broadcast([P, P]),
                                         w[:, k, cols].bitcast(F32), start=(k == 0), stop=(k == tiles - 1))
                else:
                    half, qb = divmod(i, NQ)
                    pe.wait_ge(y_free, at(b, UNITS, 1 + (qb - NQ if half else qb + NQ) + 1))
                    last = split_matmul(ps[:, 0:D], [(y_hi[:, qb, k, :], y_lo[:, qb, k, :], wo_hi[:, half * KO // 2 + k, :],
                                                      wo_lo[:, half * KO // 2 + k, :]) for k in range(KO // 2)])
                last.then_inc(job_mm, 1)

            def body(phase, b):
                for s in range(UNITS):
                    if has(phase, 0 if s >= 2 else -1):
                        transpose_probs(b, s - 2)
                    if has(phase, 0):
                        scores_of(phase, b, s, 0)
                        scores_of(phase, b, s, 1)
                    if has(phase, 0 if s >= 3 else -1):
                        outputs_of(phase, b, s - 3)
                    if has(phase, 0 if s >= 4 else -1):
                        transpose_outputs(b, s - 4)
                    if phase == DRAIN and s == 5:
                        step(0, -1)
                    for job in jobs_of(phase, s):
                        job_product(phase, b, job)

            def ternary_matmul(dst, terms, first=True, final=True):
                n = len(terms)
                for i, (a_hi, a_lo, w) in enumerate(terms):
                    pe.matmul(dst, a_hi, w, start=(first and i == 0), stop=False)
                    last = pe.matmul(dst, a_lo, w, start=False, stop=(final and i == n - 1))
                return last

            def step(n, k):
                t = k - 3
                if active(n, t):
                    pe.wait_ge(hn_ready, n * 4 + (t + 1))
                    for h in range(2):
                        pe.wait_ge(th_free, n * 8 + (2 * t + h + 1))
                        for i in range(4):
                            c = 4 * h + i
                            last = pe.transpose(ps_th[h][:, i * P:(i + 1) * P], hg[:, t % 4, c * P:(c + 1) * P],
                                                ident[:, :])
                        last.then_inc(th_mm, 1)
                t = k
                if active(n, t):
                    pe.wait_ge(tx_free, n * 4 + (1 + t + 1))
                    pe.wait_ge(z_free, n * 4 + (t + 1))
                    if k == 1:
                        pe.wait_ge(job_free, 2 + ALL_JOBS)
                    for h in range(2):
                        last = ternary_matmul(ps_z[t % 2][:, 512 * h:512 * h + 512],
                                              [(fx_hi[:, t % 2, i * P:(i + 1) * P], fx_lo[:, t % 2, i * P:(i + 1) * P],
                                                t1T[:, i, 512 * h:512 * h + 512]) for i in range(KD)])
                    last.then_inc(z_mm, 1)
                t = k + 1
                if active(n, t):
                    pe.wait_ge(xm_ready, n * 4 + (t + 1))
                    pe.wait_ge(tx_free, n * 4 + (t + 1))
                    for i in range(KD):
                        last = pe.transpose(ps_tx[:, i * P:(i + 1) * P], f_xm[:, t % 2, i * P:(i + 1) * P],
                                            ident[:, :])
                    last.then_inc(tx_mm, 1)
                t = k - 3
                if active(n, t):
                    pe.wait_ge(o_free, n * 4 + (t + 1))
                    for h in range(2):
                        pe.wait_ge(th_free, n * 8 + (2 + 2 * t + h + 1))
                        last = ternary_matmul(ps_o[:, 0:D], [(ht_hi[:, i * P:(i + 1) * P], ht_lo[:, i * P:(i + 1) * P],
                                                              t2T[:, i, :]) for i in range(4 * h, 4 * h + 4)],
                                              first=h == 0, final=h == 1)
                    last.then_inc(o_mm, 1)

            batch_ring(pe, body)
            tile_loop(pe, step, 0)


_INS = ['L0_attn_X', 'L0_attn_Wq', 'L0_attn_Wk', 'L0_attn_Wv', 'L0_attn_Wo', 'L0_ffn_ln1_g', 'L0_ffn_ln1_b',
        'L0_ffn_w1', 'L0_ffn_b1', 'L0_ffn_ln2_g', 'L0_ffn_ln2_b', 'L0_ffn_w2', 'L0_ffn_b2']
_OUTS = [((8, 512, 256), 'float32')]


def kernel(**inputs):
    import numpy as _np
    import concourse.bacc as _bacc
    from concourse import mybir as _mybir
    from concourse.bass_utils import run_bass_kernel_spmd as _run

    nc = _bacc.Bacc("TRN2", target_bir_lowering=False, num_devices=1)
    arrays, args = {}, []
    for name in _INS:
        a = _np.ascontiguousarray(inputs[name])
        arrays[f"in_{name}_dram"] = a
        args.append(nc.dram_tensor(f"in_{name}_dram", a.shape, _mybir.dt.from_np(a.dtype), kind="ExternalInput").ap())
    for i, (shape, dtype) in enumerate(_OUTS):
        dt = _mybir.dt.from_np(_np.dtype(dtype))
        args.append(nc.dram_tensor(f"out_{i}_dram", shape, dt, kind="ExternalOutput").ap())
    layer_kernel(nc, *args)
    r = _run(nc, [arrays], core_ids=[0])
    return r.results[0]["out_0_dram"]
```
